# Optimizing a Trainium2 kernel written in Bass

```python
import numpy as np
import jax
import jax.numpy as jnp

def _softmax(x, axis=-1):
    return jax.nn.softmax(x, axis=axis)

def _gelu(x):
    return jax.nn.gelu(x, approximate=True)

def _silu(x):
    return jax.nn.silu(x)

def _sigmoid(x):
    return jax.nn.sigmoid(x)

def _layernorm(x, axis=-1, eps=1e-05):
    m = jnp.mean(x, axis=axis, keepdims=True)
    v = jnp.var(x, axis=axis, keepdims=True)
    return (x - m) / jnp.sqrt(v + eps)

def _scatter_add(tgt, idx, src, axis=0):
    return tgt.at[idx].add(src)

def _segment_sum(src, seg, n):
    return jax.ops.segment_sum(src, seg, n)
kernel_name = 'mk_seq_postln_d1_jaxref_r4_1c5123'

def setup_inputs(seed: int=0):
    np.random.seed(seed)
    _w = jnp.asarray

    def _L0_attn_setup():
        import jax, jax.numpy as jnp
        import numpy as np
        EMBED_DIM = 512
        NUM_HEADS = 16
        HEAD_DIM = EMBED_DIM // NUM_HEADS
        D_K = 128
        SCALE = 1.0 / float(np.sqrt(HEAD_DIM))
        LAYER_DEPTH = 6 / 12
        BATCH, SEQ = (2, 512)
        key = jax.random.key(seed)
        ks = jax.random.split(key, 8)
        return {'hidden_states': jax.random.normal(ks[0], (BATCH, SEQ, EMBED_DIM), jnp.float32), 'c_attn_w': jax.random.normal(ks[1], (EMBED_DIM, 3 * EMBED_DIM), jnp.float32) * 0.02, 'c_attn_b': jax.random.normal(ks[2], (3 * EMBED_DIM,), jnp.float32) * 0.02, 'c_proj_w': jax.random.normal(ks[3], (EMBED_DIM, EMBED_DIM), jnp.float32) * 0.02, 'c_proj_b': jax.random.normal(ks[4], (EMBED_DIM,), jnp.float32) * 0.02, 'cam_gate': jax.random.normal(ks[5], (D_K,), jnp.float32) * 0.1, 'cam_w0': jax.random.normal(ks[6], (1,), jnp.float32), 'cam_w1': jax.random.normal(ks[7], (1,), jnp.float32)}
    _L0_attn_in = _L0_attn_setup()

    def _L0_ffn_setup():
        import jax, jax.numpy as jnp
        import numpy as np
        TOP_K = 4
        key = jax.random.key(seed)
        ks = jax.random.split(key, 9)
        B, T, D, H, NE = (2, 256, 512, 352, 16)
        s = 0.02
        return {'x': jax.random.normal(ks[0], (B, T, D), jnp.float32), 'gate_w': jax.random.normal(ks[1], (NE, D), jnp.float32) * s, 'gate_b': jax.random.normal(ks[2], (NE,), jnp.float32) * s, 'w1_shared': jax.random.normal(ks[3], (D, H), jnp.float32) * s, 'w2_shared': jax.random.normal(ks[4], (H, D), jnp.float32) * s, 'w3_shared': jax.random.normal(ks[5], (D, H), jnp.float32) * s, 'w1_routed': jax.random.normal(ks[6], (NE, D, H), jnp.float32) * s, 'w2_routed': jax.random.normal(ks[7], (NE, H, D), jnp.float32) * s, 'w3_routed': jax.random.normal(ks[8], (NE, D, H), jnp.float32) * s}
    _L0_ffn_in = _L0_ffn_setup()
    _d = {'L0_attn_hidden_states': _L0_attn_in['hidden_states'], 'L0_attn_c_attn_w': _L0_attn_in['c_attn_w'], 'L0_attn_c_attn_b': _L0_attn_in['c_attn_b'], 'L0_attn_c_proj_w': _L0_attn_in['c_proj_w'], 'L0_attn_c_proj_b': _L0_attn_in['c_proj_b'], 'L0_attn_cam_gate': _L0_attn_in['cam_gate'], 'L0_attn_cam_w0': _L0_attn_in['cam_w0'], 'L0_attn_cam_w1': _L0_attn_in['cam_w1'], 'L0_ffn_gate_w': _L0_ffn_in['gate_w'], 'L0_ffn_gate_b': _L0_ffn_in['gate_b'], 'L0_ffn_w1_shared': _L0_ffn_in['w1_shared'], 'L0_ffn_w2_shared': _L0_ffn_in['w2_shared'], 'L0_ffn_w3_shared': _L0_ffn_in['w3_shared'], 'L0_ffn_w1_routed': _L0_ffn_in['w1_routed'], 'L0_ffn_w2_routed': _L0_ffn_in['w2_routed'], 'L0_ffn_w3_routed': _L0_ffn_in['w3_routed']}
    _x0 = _d['L0_attn_hidden_states']
    _d['L0_attn_hidden_states'] = jax.random.normal(jax.random.fold_in(jax.random.key(seed), 1), (2, 1024, 512), dtype=_x0.dtype)
    del _x0
    return _d

def reference(L0_attn_hidden_states, L0_attn_c_attn_w, L0_attn_c_attn_b, L0_attn_c_proj_w, L0_attn_c_proj_b, L0_attn_cam_gate, L0_attn_cam_w0, L0_attn_cam_w1, L0_ffn_gate_w, L0_ffn_gate_b, L0_ffn_w1_shared, L0_ffn_w2_shared, L0_ffn_w3_shared, L0_ffn_w1_routed, L0_ffn_w2_routed, L0_ffn_w3_routed):

    def _L0_attn_ref(hidden_states, c_attn_w, c_attn_b, c_proj_w, c_proj_b, cam_gate, cam_w0, cam_w1):
        import jax, jax.numpy as jnp
        import numpy as np
        EMBED_DIM = 512
        NUM_HEADS = 16
        HEAD_DIM = EMBED_DIM // NUM_HEADS
        D_K = 128
        SCALE = 1.0 / float(np.sqrt(HEAD_DIM))
        LAYER_DEPTH = 6 / 12
        BATCH, SEQ = (2, 512)
        qkv = hidden_states @ c_attn_w + c_attn_b
        Q, K, V = jnp.split(qkv, 3, axis=2)
        attn_scores = jnp.einsum('bse,bte->bst', Q, K) * SCALE
        Q_cam, K_cam, V_cam = (Q[:, :, :D_K], K[:, :, :D_K], V[:, :, :D_K])
        base_A = jax.lax.stop_gradient(jax.nn.softmax(jnp.einsum('bsd,btd->bst', Q_cam, K_cam) * SCALE, axis=-1))
        layer_weight = jax.nn.sigmoid(cam_w0[0] + cam_w1[0] * LAYER_DEPTH)
        cam_ctx = jnp.einsum('bst,btd->bsd', base_A, V_cam)
        cam_bias = jnp.einsum('bsd,btd->bst', jnp.tanh(cam_ctx * cam_gate), K_cam)
        cam_bias = cam_bias * (SCALE * layer_weight)
        final_attn = jax.nn.softmax(attn_scores + cam_bias, axis=-1)
        context = jnp.einsum('bst,bte->bse', final_attn, V)
        output = context @ c_proj_w + c_proj_b
        return output

    def _L0_ffn_ref(x, gate_w, gate_b, w1_shared, w2_shared, w3_shared, w1_routed, w2_routed, w3_routed):
        import jax, jax.numpy as jnp
        import numpy as np
        TOP_K = 4
        n_experts = w1_routed.shape[0]
        logits = jnp.einsum('ed,btd->bte', gate_w, x)
        scores = jax.nn.sigmoid(logits) + gate_b
        weights, indices = jax.lax.top_k(scores, TOP_K)
        weights = weights / weights.sum(-1, keepdims=True)
        shared_out = jax.nn.silu(x @ w1_shared) * (x @ w3_shared) @ w2_shared
        one_hot = jax.nn.one_hot(indices, n_experts, dtype=x.dtype)
        router_probs = (weights[..., None] * one_hot).sum(-2)
        h1 = jnp.einsum('btd,edc->btec', x, w1_routed)
        h2 = jnp.einsum('btd,edc->btec', x, w3_routed)
        h3 = jax.nn.silu(h1 * h2)
        experts_out = jnp.einsum('btec,ecd->bted', h3, w2_routed)
        routed_out = jnp.einsum('bted,bte->btd', experts_out, router_probs)
        return shared_out + routed_out
    x = L0_attn_hidden_states
    x = _layernorm(x + _L0_attn_ref(x, L0_attn_c_attn_w, L0_attn_c_attn_b, L0_attn_c_proj_w, L0_attn_c_proj_b, L0_attn_cam_gate, L0_attn_cam_w0, L0_attn_cam_w1), axis=-1)
    x = _layernorm(x + _L0_ffn_ref(x, L0_ffn_gate_w, L0_ffn_gate_b, L0_ffn_w1_shared, L0_ffn_w2_shared, L0_ffn_w3_shared, L0_ffn_w1_routed, L0_ffn_w2_routed, L0_ffn_w3_routed), axis=-1)
    return x

_drawn_inputs = setup_inputs


def setup_inputs(seed=0):
    import zlib

    import numpy as np

    out = dict(_drawn_inputs(seed))
    spreads = {}
    factors = {'L0_attn_c_attn_w': 4.915,
     'L0_attn_c_attn_b': 6.225,
     'L0_attn_c_proj_w': 3.892,
     'L0_attn_c_proj_b': 2.858,
     'L0_attn_cam_gate': 8.0,
     'L0_ffn_gate_w': 3.292,
     'L0_ffn_gate_b': 7.908,
     'L0_ffn_w1_routed': 2.875,
     'L0_ffn_w2_routed': 2.834,
     'L0_ffn_w3_routed': 2.873}
    for name, (base, spread) in spreads.items():
        noise = np.random.default_rng([zlib.crc32(name.encode()), seed]).standard_normal(out[name].shape)
        drawn = base * np.exp(spread * noise) if base else spread * noise
        out[name] = jnp.asarray(drawn.astype(out[name].dtype))
    for name, factor in factors.items():
        out[name] = (out[name] * factor).astype(out[name].dtype)
    return out
```

```python
import concourse.bass as bass
from concourse import mybir
from contextlib import ExitStack



def post_ln_attention_moe_kernel(
    nc, hidden_states, c_attn_w, c_attn_b, c_proj_w, c_proj_b, cam_gate, cam_w0, cam_w1,
    gate_w, gate_b, w1_shared, w2_shared, w3_shared, w1_routed, w2_routed, w3_routed,
    router_dram, vproj_dram, out,
):
    f32 = mybir.dt.float32
    f32r = mybir.dt.float32r
    ALU = mybir.AluOpType
    ACT = mybir.ActivationFunctionType
    AX = mybir.AxisListType

    P = 128
    BATCH, SEQ, D = hidden_states.shape
    KD = D // P
    TB = SEQ // P
    TILES = BATCH * TB
    BLK = 512
    TPB = BLK // P
    NBB = SEQ // BLK
    NBLK = BATCH * NBB
    DCAM = cam_gate.shape[0]
    SCALE = 1.0 / float(32) ** 0.5
    NE, _, HID = w1_routed.shape
    HSH = w1_shared.shape[1]
    TOPK = 4
    EPS = 1e-5
    assert DCAM == P

    SB = 4
    CH = SB * HID // P
    ITERS = NE // SB
    GROUPS = [(0, [0, 1]), (2, [3, 4, 5]), (5, [0, 1, 2]), (8, [3, 4, 5])]
    NSLOT = 6
    SHC = -(-HSH // P)
    SH_SLOTS = [3, 4, 5]
    SHU = SHC * NBLK
    ITU = CH * NBLK

    def pieces(j):
        res, r = [], 0
        while r < P:
            e, c = divmod(P * j + r, HID)
            n = min(P - r, HID - c)
            res.append((e, c, r, n))
            r += n
        return res

    x_tiles = hidden_states.rearrange("b (t p) d -> (b t) p d", p=P)
    out_tiles = out.rearrange("b (t p) d -> (b t) p d", p=P)
    wqkv = c_attn_w.rearrange("(k p) n -> p k n", p=P)
    bqkv = c_attn_b.rearrange("(m p) -> p m", p=P)
    wp_v = c_proj_w.rearrange("(k p) n -> p k n", p=P)
    w1s = w1_shared.rearrange("(k p) h -> p k h", p=P)
    w3s = w3_shared.rearrange("(k p) h -> p k h", p=P)
    w1r = w1_routed.rearrange("e (k p) h -> e p k h", p=P)
    w3r = w3_routed.rearrange("e (k p) h -> e p k h", p=P)
    w2r = w2_routed.rearrange("e h d -> (e h) d")

    ctx = ExitStack()
    with ctx:
        def sb(name, shape, dt=f32):
            return ctx.enter_context(nc.sbuf_tensor(name, shape, dt))

        def sem(name):
            return ctx.enter_context(nc.semaphore(name))

        ps = ctx.enter_context(nc.psum_tensor("ps", [P, 8 * BLK], f32))

        def bank(i, n=1):
            return ps[:, i * BLK:(i + n) * BLK]

        R = sb("R", [P, 36 * 1024], f32r)
        acc = sb("acc", [P, TILES, D])
        scratch = sb("scratch", [P, 8 * BLK])
        raw = sb("raw", [P, 3, BLK])
        xst = sb("xst", [P, 2, D])
        crow = sb("crow", [P, D])
        ident = sb("ident", [P, P])
        bcol = sb("bcol", [P, 3 * KD])
        gcol = sb("gcol", [P, 1])
        gbv = sb("gbv", [P, 1])
        w0c = sb("w0c", [P, 1])
        w1c = sb("w1c", [P, 1])
        lw = sb("lw", [P, 4])
        ones = sb("ones", [P, 1])
        stat = sb("stat", [P, 8, TILES])
        bst = sb("bst", [P, TILES, 6])
        bag = sb("bag", [P, TILES, 2])
        rstd = sb("rstd", [P, 3, TILES])
        GWT = sb("GWT", [P, 2, KD, NE], f32r)
        gb = sb("gb", [P, NE])

        def view(off, *dims):
            n = 1
            for d in dims:
                n *= d
            v = R[:, off:off + n]
            if len(dims) == 2:
                return v.rearrange("p (a b) -> p a b", a=dims[0])
            return v.rearrange("p (a b c) -> p a b c", a=dims[0], b=dims[1])

        XT = view(0, 2, KD, SEQ)
        KT = view(8192, 2, KD, SEQ)
        QT = view(16384, 2, KD, SEQ)
        WVP = view(16384, 2, KD, D)
        VW = view(24576, 2, TB, D)
        VC = view(32768, 2, TB, DCAM)
        WS = [view(34816 + 1024 * s, 2, KD, P) for s in range(2)]
        PTB = [view(1024 * s, 2, BLK) for s in range(2)]
        PTF = [view(2048 * (1 + s), 2, TB, P) for s in range(2)]
        WVT = view(8192, 2, KD, D)
        WPR = view(12288, 2, KD, D)
        BVB = view(24576, 2, KD, P)
        X1T = view(0, 2, KD, SEQ * BATCH)
        W1 = [view(16384 + 3072 * s, 2, KD, P) for s in range(NSLOT)]
        W3 = [view(17408 + 3072 * s, 2, KD, P) for s in range(NSLOT)]
        W2 = [view(18432 + 3072 * s, 2, D) for s in range(NSLOT)]
        HB = [view(34816 + 1024 * s, 2, BLK) for s in range(2)]

        probs = scratch[:, :].rearrange("p (s t) -> p s t", s=4)
        wv_raw = scratch[:, 0:4 * BLK].rearrange("p (k n) -> p k n", k=KD)
        wp_raw = scratch[:, 4 * BLK:8 * BLK].rearrange("p (k n) -> p k n", k=KD)
        ub = scratch[:, 0:4 * BLK].rearrange("p (s t) -> p s t", s=4)
        pb = scratch[:, 4 * BLK:8 * BLK].rearrange("p (s t) -> p s t", s=4)
        cmp_a = scratch[:, 4 * BLK:6 * BLK].rearrange("p (t e j) -> p t e j", t=TPB, e=NE)
        cmp_b = scratch[:, 6 * BLK:8 * BLK].rearrange("p (t e j) -> p t e j", t=TPB, e=NE)
        prT = pb[0:NE]
        gw = raw[0:NE, 2, :]
        tcam, qfull = raw[:, 1, :], raw[:, 2, :]
        sc = xst[:, 0, 0:256].rearrange("p (t e) -> p t e", t=TILES)
        rk = xst[:, 0, 256:512].rearrange("p (t e) -> p t e", t=TILES)
        pr = xst[:, 1, 0:256].rearrange("p (t e) -> p t e", t=TILES)
        below = xst[:, 1, 256:512].rearrange("p (e j) -> p e j", e=NE)
        wsum = stat[:, 0, :]
        winv = stat[:, 1, :]

        const_ld = sem("const_ld")
        acc_ld = sem("acc_ld")
        xst_ld = [sem(f"xst_ld{s}") for s in range(2)]
        raw_ld = [sem(f"raw_ld{s}") for s in range(3)]
        id_step = sem("id_step")
        wp_hi, wp_lo = sem("wp_hi"), sem("wp_lo")
        w_hi, w_lo = sem("w_hi"), sem("w_lo")
        wvt_ps, wvt_hi, wvt_lo = sem("wvt_ps"), sem("wvt_hi"), sem("wvt_lo")
        bvb_hi, bvb_lo = sem("bvb_hi"), sem("bvb_lo")
        wvp_ps, wvp_cp, wvp_st = sem("wvp_ps"), sem("wvp_cp"), sem("wvp_st")
        crow_ps, crow_ok = sem("crow_ps"), sem("crow_ok")
        lw_v, lw_e = sem("lw_v"), sem("lw_e")
        gbv_ok = sem("gbv_ok")
        xt_ps, xt_hi, xt_lo = sem("xt_ps"), sem("xt_hi"), sem("xt_lo")
        qk_ps, qk_hi, qk_lo = sem("qk_ps"), sem("qk_hi"), sem("qk_lo")
        vc_ps, vc_hi, vc_lo = sem("vc_ps"), sem("vc_hi"), sem("vc_lo")
        vw_ps, vw_hi, vw_lo = sem("vw_ps"), sem("vw_hi"), sem("vw_lo")
        bs_ps, bs_mx, bs_nm, bs_ex, bs_ri, bs_no = (sem(f"bs_{n}") for n in ("ps", "mx", "nm", "ex", "ri", "no"))
        bt_ps, bt_hi, bt_lo, bc_mm = sem("bt_ps"), sem("bt_hi"), sem("bt_lo"), sem("bc_mm")
        tc_ok, qf_ok, qn_ok, qc_hi, qc_lo = sem("tc_ok"), sem("qf_ok"), sem("qn_ok"), sem("qc_hi"), sem("qc_lo")
        fs_ps, fs_mx, fs_nm, fs_ex, fs_ri = (sem(f"fs_{n}") for n in ("ps", "mx", "nm", "ex", "ri"))
        ft_ps, ft_hi, ft_lo, fo_mm = sem("ft_ps"), sem("ft_hi"), sem("ft_lo"), sem("fo_mm")
        xc_ok, res_ok, bst_ok, bag_ok = sem("xc_ok"), sem("res_ok"), sem("bst_ok"), sem("bag_ok")
        ve_ok, sq_ok, rs_ok, nm_ok = sem("ve_ok"), sem("sq_ok"), sem("rs_ok"), sem("nm_ok")
        x1_ok, x1t_ps, x1t_hi, x1t_lo = sem("x1_ok"), sem("x1t_ps"), sem("x1t_hi"), sem("x1t_lo")
        gt_ps, gt_hi, gt_lo, lg_ps, lg_sg = sem("gt_ps"), sem("gt_hi"), sem("gt_lo"), sem("lg_ps"), sem("lg_sg")
        rt_step, below_ok, pr_ok, pt_ps, pt_cp, pt_st = (sem(n) for n in ("rt_step", "below_ok", "pr_ok", "pt_ps", "pt_cp", "pt_st"))
        wraw_ld = [sem(f"wraw_ld{s}") for s in range(3)]
        pad_ok = sem("pad_ok")
        fw_hi, fw_lo = sem("fw_hi"), sem("fw_lo")
        pb_ld = [sem(f"pb_ld{s}") for s in range(4)]
        h_mm, h1_cp, z_ok, silu_ok, h3_ok, hb_hi, hb_lo, o_mm, acc_ok = (
            sem(n) for n in ("h_mm", "h1_cp", "z_ok", "silu_ok", "h3_ok", "hb_hi", "hb_lo", "o_mm", "acc_ok"))
        out_ok, out_st = sem("out_ok"), sem("out_st")

        SMALL = 10
        WUNITS = 4 * KD - 3

        def unit_k(b, m):
            return WUNITS * b + m

        def unit_vc(b):
            return WUNITS * b + KD

        def unit_wvp(b, k):
            return WUNITS * b + KD + 1 + k

        def unit_q(b, m):
            return WUNITS * b + 2 * KD + 1 + m

        def ring_no(b, i):
            return (2 * KD + 1) * b + i

        def terms(lhs, rhs):
            return [(lhs(0), rhs(0)), (lhs(0), rhs(1)), (lhs(1), rhs(0))]

        block = ctx.enter_context(nc.Block())

        @block.sync
        def _(sp):
            sp.dma_start(wv_raw, wqkv[:, :, 2 * D:3 * D]).then_inc(const_ld, 16)
            sp.dma_start(wp_raw, wp_v).then_inc(const_ld, 16)
            sp.dma_start(bcol[:, :], bqkv, allow_slow_non_contiguous=True).then_inc(const_ld, 16)
            sp.dma_start(gcol[:, :], cam_gate.rearrange("(p a) -> p a", a=1)).then_inc(const_ld, 16)
            sp.dma_start(w0c[:, :], cam_w0.rearrange("(a n) -> a n", a=1).to_broadcast([P, 1])).then_inc(const_ld, 16)
            sp.dma_start(w1c[:, :], cam_w1.rearrange("(a n) -> a n", a=1).to_broadcast([P, 1])).then_inc(const_ld, 16)
            sp.dma_start(crow[:, :], c_proj_b.rearrange("(a n) -> a n", a=1).to_broadcast([P, D])).then_inc(const_ld, 16)
            sp.dma_start(gw, gate_w).then_inc(const_ld, 16)
            sp.dma_start(gb[:, :], gate_b.rearrange("(a n) -> a n", a=1).to_broadcast([P, NE])).then_inc(const_ld, 16)

            def load_x(g):
                if g >= 2:
                    sp.wait_ge(xt_ps, g - 1)
                sp.dma_start(xst[:, g % 2, :], x_tiles[g]).then_inc(xst_ld[g % 2], 16)

            def load_raw(n, src):
                if n == 2:
                    sp.wait_ge(gt_ps, 1)
                if n >= 3:
                    sp.wait_ge(w_lo, n - 2)
                dst = raw[:, n % 3, :]
                if len(src.shape) == 3:
                    dst = dst.rearrange("p (k n) -> p k n", k=KD)
                sp.dma_start(dst, src).then_inc(raw_ld[n % 3], 16)

            for b in range(BATCH):
                if b:
                    sp.wait_ge(qc_lo, NBB * b)
                load_x(b * TB)
                load_x(b * TB + 1)
                early = 3 if b == 0 else 0
                for m in range(early):
                    load_raw(unit_k(b, m), wqkv[:, :, D + m * P:D + (m + 1) * P])
                if b == 0:
                    for k in range(KD):
                        sp.wait_ge(wvp_cp, k + 1)
                        sp.dma_start(vproj_dram[k * P:(k + 1) * P, :], probs[:, k % 2, 0:D]).then_inc(wvp_st, 16)
                        sp.wait_ge(wvp_st, 16 * (k + 1))
                    sp.dma_start(acc[:, :, :], x_tiles.rearrange("t p d -> p t d")).then_inc(acc_ld, 16)
                for t in range(2, TB):
                    load_x(b * TB + t)
                for m in range(early, KD):
                    load_raw(unit_k(b, m), wqkv[:, :, D + m * P:D + (m + 1) * P])
                load_raw(unit_vc(b), wqkv[:, :, 2 * D:2 * D + DCAM])
                for k in range(KD):
                    load_raw(unit_wvp(b, k), vproj_dram[k * P:(k + 1) * P, :])
                for m in range(KD):
                    load_raw(unit_q(b, m), wqkv[:, :, m * P:(m + 1) * P])

            def load_chunk(cs, j, e0):
                free = 3 * cs
                for kind, wsrc in ((0, w1r), (1, w3r)):
                    sp.wait_ge(fw_lo, free + kind - 2)
                    dst = raw[:, kind, :].rearrange("p (k n) -> p k n", k=KD)
                    for e, c, r, n in pieces(j):
                        sp.dma_start(dst[:, :, r:r + n], wsrc[bass.ds(e0 + e, 1), :, :, c:c + n].rearrange(
                            "e p k h -> (e p) k h")).then_inc(wraw_ld[kind], 16)
                sp.wait_ge(fw_lo, free)
                sp.dma_start(raw[:, 2, :], w2r[bass.ds(e0 * HID + j * P, P), :]).then_inc(wraw_ld[2], 16)

            sp.wait_ge(qc_lo, NBLK)
            for c in range(SHC):
                n = min(P, HSH - c * P)
                for kind, wsrc in ((0, w1s), (1, w3s)):
                    if c:
                        sp.wait_ge(fw_lo, 3 * c + kind - 2)
                    dst = raw[:, kind, :].rearrange("p (k n) -> p k n", k=KD)
                    sp.dma_start(dst[:, :, 0:n], wsrc[:, :, c * P:c * P + n]).then_inc(wraw_ld[kind], 16)
                if c:
                    sp.wait_ge(fw_lo, 3 * c)
                sp.dma_start(raw[0:n, 2, :], w2_shared[c * P:c * P + n, :]).then_inc(wraw_ld[2], 16)
            for nb in range(NBLK):
                sp.wait_ge(pt_cp, nb + 1)
                sp.dma_start(router_dram[:, nb * BLK:(nb + 1) * BLK], prT[:, nb, :]).then_inc(pt_st, 16)
            sp.wait_ge(pt_st, 16 * NBLK)


            with nc.sync.Fori(0, ITERS) as it:
                for first, slots in GROUPS:
                    u0 = first * NBLK
                    size = len(slots)
                    for c in range(size):
                        load_chunk(SHC + it * CH + first + c, first + c, it * SB)
                    for nb in range(NBLK):
                        for c in range(size):
                            k = u0 + nb * size + c
                            sp.wait_ge(h3_ok, it * ITU + (SHU + k - 3))
                            for e, _, r, n in pieces(first + c):
                                src = router_dram[bass.ds(it * SB + e, 1), nb * BLK:(nb + 1) * BLK]
                                sp.dma_start(pb[r:r + n, k % 4, :], src.to_broadcast([n, BLK])).then_inc(pb_ld[k % 4], 16)
            for t in range(TILES):
                sp.wait_ge(out_ok, t + 1)
                sp.dma_start(out_tiles[t], acc[:, t, :]).then_inc(out_st, 16)
            sp.wait_ge(out_st, 16 * TILES)

        @block.gpsimd
        def _(pool):
            nc.gpsimd.memset(ident[:, :], 0.0).then_inc(id_step, 1)
            pool.wait_ge(id_step, 1)
            nc.gpsimd.affine_select(out=ident[:, :], in_=ident[:, :], compare_op=ALU.not_equal, fill=1.0, base=0,
                                    pattern=[[-1, P]], channel_multiplier=1).then_inc(id_step, 1)
            pool.wait_ge(const_ld, 16 * (SMALL - 1))
            nc.gpsimd.tensor_copy(WPR[:, 0], wp_raw).then_inc(wp_hi, 1)
            pool.wait_ge(wp_hi, 1)
            nc.gpsimd.tensor_tensor(WPR[:, 1], wp_raw, WPR[:, 0].bitcast(f32), ALU.subtract).then_inc(wp_lo, 1)

            def split(n, src, hi, lo):
                pool.wait_ge(raw_ld[n % 3], 16 * (n // 3 + 1))
                nc.gpsimd.tensor_copy(hi, src).then_inc(w_hi, 1)
                pool.wait_ge(w_hi, n + 1)
                nc.gpsimd.tensor_tensor(lo, src, hi.bitcast(f32), ALU.subtract).then_inc(w_lo, 1)

            def split_ring(b, i, n):
                ws = WS[ring_no(b, i) % 2]
                split(n, raw[:, n % 3, :].rearrange("p (k n) -> p k n", k=KD), ws[:, 0], ws[:, 1])

            for b in range(BATCH):
                for m in range(KD):
                    i = m
                    if m >= 2:
                        pool.wait_ge(qk_ps, 16 * b + 2 * (m - 1))
                    elif b:
                        pool.wait_ge(qk_ps, 16 * b)
                    split_ring(b, i, unit_k(b, m))
                pool.wait_ge(qk_ps, 16 * b + 2 * (KD - 1))
                split_ring(b, KD, unit_vc(b))
                if b:
                    pool.wait_ge(fo_mm, TB * b)
                for k in range(KD):
                    n = unit_wvp(b, k)
                    split(n, raw[:, n % 3, :], WVP[:, 0, k, :], WVP[:, 1, k, :])
                for m in range(KD):
                    if m == 0:
                        pool.wait_ge(qk_ps, 16 * b + 2 * KD)
                    elif m == 1:
                        pool.wait_ge(vc_ps, 2 * b + 2)
                    else:
                        pool.wait_ge(qk_ps, 16 * b + 2 * KD + 2 * (m - 1))
                    split_ring(b, KD + 1 + m, unit_q(b, m))
                if b == 0:
                    pool.wait_ge(acc_ld, 16)
                    pool.wait_ge(crow_ok, 1)
                    for t in range(TILES):
                        nc.gpsimd.tensor_tensor(acc[:, t, :], acc[:, t, :], crow[:, :], ALU.add).then_inc(xc_ok, 1)
                for i in range(TB):
                    g = TB * b + i
                    pool.wait_ge(bs_ri, g + 1)
                    nc.gpsimd.tensor_scalar(probs[:, i % 4, :], probs[:, i % 4, :], stat[:, 3, g:g + 1], None,
                                            ALU.mult).then_inc(bs_no, 1)

            pool.wait_ge(xt_ps, TILES)
            pool.wait_ge(fo_mm, TILES)
            nc.gpsimd.memset(ones[:, :], 1.0).then_inc(pad_ok, 1)
            pool.wait_ge(pad_ok, 1)
            nc.gpsimd.memset(below, 1.0).then_inc(below_ok, 1)
            pool.wait_ge(below_ok, 1)
            nc.gpsimd.affine_select(out=below, in_=below, compare_op=ALU.is_gt, fill=0.0, base=0,
                                    pattern=[[1, NE], [-1, NE]], channel_multiplier=0).then_inc(below_ok, 1)

            def split_ffn(n, src, dst):
                one = ones[:, :].to_broadcast([P, BLK])
                if len(src.shape) == 3:
                    one = one.rearrange("p (k n) -> p k n", k=KD)
                nc.gpsimd.tensor_tensor(dst[:, 0], src, one, ALU.mult).then_inc(fw_hi, 1)
                pool.wait_ge(fw_hi, n + 1)
                nc.gpsimd.tensor_tensor(dst[:, 1], src, dst[:, 0].bitcast(f32), ALU.subtract).then_inc(fw_lo, 1)

            def split_chunk(cs, slot, arrived):
                for kind, dst in ((0, W1[slot]), (1, W3[slot]), (2, W2[slot])):
                    pool.wait_ge(wraw_ld[kind], arrived[kind])
                    src = raw[:, kind, :]
                    if kind < 2:
                        src = src.rearrange("p (k n) -> p k n", k=KD)
                    split_ffn(3 * cs + kind, src, dst)

            for c in range(SHC):
                if c == SHC - 1 and HSH % P:
                    pool.wait_ge(fw_lo, 3 * c)
                    for kind in range(2):
                        nc.gpsimd.memset(raw[:, kind, :].rearrange("p (k n) -> p k n", k=KD)[:, :, HSH % P:P],
                                         0.0).then_inc(pad_ok, 1)
                    pool.wait_ge(pad_ok, 3)
                    nc.gpsimd.memset(raw[HSH % P:P, 2, :], 0.0).then_inc(pad_ok, 1)
                    pool.wait_ge(pad_ok, 4)
                split_chunk(c, SH_SLOTS[c], [16 * (c + 1)] * 3)

            per_it = [sum(len(pieces(j)) for j in range(CH))] * 2 + [CH]
            with nc.gpsimd.Fori(0, ITERS) as it:
                sofar = [0, 0, 0]
                for gi, (first, slots) in enumerate(GROUPS):
                    done = it * ITU + (1, SHU, SHU + GROUPS[1][0] * NBLK, SHU + GROUPS[2][0] * NBLK)[gi]
                    pool.wait_ge(o_mm, done)
                    for c, slot in enumerate(slots):
                        n = len(pieces(first + c))
                        sofar = [sofar[0] + n, sofar[1] + n, sofar[2] + 1]
                        split_chunk(SHC + it * CH + first + c, slot,
                                    [it * (16 * per_it[k]) + 16 * (SHC + sofar[k]) for k in range(3)])

        @block.scalar
        def _(act):
            act.wait_ge(lw_v, 1)
            nc.scalar.activation(lw[:, 1:2], lw[:, 0:1], ACT.Exp, scale=-1.0).then_inc(lw_e, 1)
            for k in range(KD):
                act.wait_ge(wvt_ps, k + 1)
                nc.scalar.activation(WVT[:, 0, k, :], bank(k), ACT.Copy).then_inc(wvt_hi, 1)
            for k in range(KD):
                act.wait_ge(wvp_ps, k + 1)
                if k >= 2:
                    act.wait_ge(wvp_st, 16 * (k - 1))
                nc.scalar.activation(probs[:, k % 2, 0:D], bank(4 + k % 2), ACT.Copy).then_inc(wvp_cp, 1)

            def hi_copy(ready, count, dst, src, done, bias=None):
                act.wait_ge(ready, count)
                if bias is None:
                    nc.scalar.activation(dst, src, ACT.Copy).then_inc(done, 1)
                else:
                    nc.scalar.activation(dst, src, ACT.Identity, bias=bias).then_inc(done, 1)

            hi_copy(gt_ps, 1, GWT[:, 0], bank(7)[:, 0:KD * NE].rearrange("p (k e) -> p k e", k=KD), gt_hi)
            for b in range(BATCH):
                for t in range(TB):
                    g = TB * b + t
                    hi_copy(xt_ps, g + 1, XT[:, 0, :, t * P:(t + 1) * P], bank(g % 2).rearrange("p (k t) -> p k t", k=KD), xt_hi)
                for m in range(KD):
                    for h in range(NBB):
                        q = 16 * b + 2 * m + h
                        hi_copy(qk_ps, q + 1, KT[:, 0, m, h * BLK:(h + 1) * BLK], bank(2 + q % 2), qk_hi,
                                bcol[:, KD + m:KD + m + 1])
                for c in range(2):
                    hi_copy(vc_ps, 2 * b + c + 1, VC[:, 0, 4 * c:4 * c + 4, :],
                            bank(4 + c).rearrange("p (t d) -> p t d", t=4), vc_hi)
                for t in range(TB):
                    g = TB * b + t
                    hi_copy(vw_ps, g + 1, VW[:, 0, t, :], bank(6 + g % 2), vw_hi)
                for m in range(KD):
                    for h in range(NBB):
                        q = 16 * b + 8 + 2 * m + h
                        hi_copy(qk_ps, q + 1, QT[:, 0, m, h * BLK:(h + 1) * BLK], bank(2 + q % 2), qk_hi,
                                bcol[:, m:m + 1])
                for n in range(NBB):
                    B = NBB * b + n
                    for i in range(4):
                        g = 4 * B + i
                        act.wait_ge(bs_nm, g + 1)
                        if n:
                            act.wait_ge(bt_ps, 8 * B)
                        nc.scalar.activation(probs[:, i, :], bank(2 * (g % 2), 2), ACT.Exp, bias=stat[:, 1, g:g + 1],
                                             scale=SCALE, accum_out=stat[:, 2, g:g + 1]).then_inc(bs_ex, 1)
                    for j in range(TB):
                        k = TB * B + j
                        if k >= 2:
                            act.wait_ge(bc_mm, k - 1)
                        hi_copy(bt_ps, k + 1, PTB[j % 2][:, 0, :], bank(4 + j % 2), bt_hi)
                    act.wait_ge(bc_mm, TB * B + TB)
                    act.wait_ge(gbv_ok, 1)
                    act.wait_ge(w_lo, WUNITS * (b + 1))
                    if n:
                        act.wait_ge(qn_ok, B)
                    nc.scalar.activation(tcam, bank(6), ACT.Tanh, bias=gbv[:, 0:1], scale=gcol[:, 0:1]).then_inc(tc_ok, 1)
                    act.wait_ge(qn_ok, B + 1)
                    nc.scalar.activation(QT[:, 0, 0, n * BLK:(n + 1) * BLK], qfull, ACT.Copy).then_inc(qc_hi, 1)
                def exp_final(g):
                    i = g % TB
                    act.wait_ge(fs_nm, g + 1)
                    if i >= 4:
                        act.wait_ge(ft_ps, 2 * (g - 3))
                    nc.scalar.activation(probs[:, i % 4, :], bank(0, 2), ACT.Exp, bias=stat[:, 5, g:g + 1],
                                         scale=SCALE, accum_out=stat[:, 6, g:g + 1]).then_inc(fs_ex, 1)

                exp_final(TB * b)
                for i in range(TB):
                    g = TB * b + i
                    for c in range(2):
                        if i >= 2:
                            act.wait_ge(fo_mm, g - 1)
                        hi_copy(ft_ps, 2 * g + c + 1, PTF[g % 2][:, 0, 4 * c:4 * c + 4, :],
                                bank(2 + c).rearrange("p (t d) -> p t d", t=4), ft_hi)
                    if i < TB - 1:
                        exp_final(g + 1)

            act.wait_ge(ve_ok, 1)
            nc.scalar.activation(rstd[:, 1, :], rstd[:, 0, :], ACT.Sqrt).then_inc(sq_ok, 1)
            for t in range(TILES):
                hi_copy(x1t_ps, t + 1, X1T[:, 0, :, t * P:(t + 1) * P], bank(t % 4).rearrange("p (k t) -> p k t", k=KD), x1t_hi)
            act.wait_ge(lg_ps, 1)
            nc.scalar.activation(sc, bank(4)[:, 0:TILES * NE].rearrange("p (t e) -> p t e", t=TILES),
                                 ACT.Sigmoid).then_inc(lg_sg, 1)

            def shared_unit(u):
                act.wait_ge(h_mm, u + 1)
                if u >= 4:
                    act.wait_ge(hb_lo, u - 3)
                nc.scalar.activation(ub[:, u % 4, :], bank(2 * (u % 2)), ACT.Silu).then_inc(h1_cp, 1)
                act.wait_ge(h3_ok, u + 1)
                if u >= 2:
                    act.wait_ge(o_mm, u - 1)
                nc.scalar.activation(HB[u % 2][:, 0, :], ub[:, u % 4, :], ACT.Copy).then_inc(hb_hi, 1)
                if u >= 8:
                    nb = u - 8
                    act.wait_ge(pt_ps, nb + 1)
                    nc.scalar.activation(prT[:, nb, :], bank(2 * ((nb + 1) % 2))[0:NE, :], ACT.Copy).then_inc(pt_cp, 1)

            def routed_unit(it, k):
                u = it * ITU + (SHU + k)
                act.wait_ge(h_mm, u + 1)
                act.wait_ge(hb_lo, u - 3)
                nc.scalar.activation(ub[:, k % 4, :], bank(2 * (k % 2)), ACT.Copy).then_inc(h1_cp, 1)
                act.wait_ge(z_ok, it * ITU + (k + 1))
                nc.scalar.activation(ub[:, k % 4, :], ub[:, k % 4, :], ACT.Silu).then_inc(silu_ok, 1)
                act.wait_ge(h3_ok, u + 1)
                act.wait_ge(o_mm, u - 1)
                nc.scalar.activation(HB[k % 2][:, 0, :], ub[:, k % 4, :], ACT.Copy).then_inc(hb_hi, 1)

            for u in range(SHU):
                shared_unit(u)
            with nc.scalar.Fori(0, ITERS) as it:
                for k in range(ITU):
                    routed_unit(it, k)
            act.wait_ge(ve_ok, 2)
            nc.scalar.activation(rstd[:, 1, :], rstd[:, 0, :], ACT.Sqrt).then_inc(sq_ok, 1)

        @block.vector
        def _(dve):
            dve.wait_ge(const_ld, 16 * (SMALL - 1))
            nc.vector.scalar_tensor_tensor(lw[:, 0:1], w1c[:, :], 0.5, w0c[:, :], ALU.mult, ALU.add).then_inc(lw_v, 1)
            nc.vector.tensor_tensor(gbv[:, :], gcol[:, :], bcol[:, 2 * KD:2 * KD + 1], ALU.mult).then_inc(gbv_ok, 1)
            bvb = bcol[:, 2 * KD:3 * KD].unsqueeze(2).to_broadcast([P, KD, P])
            nc.vector.tensor_copy(BVB[:, 0], bvb).then_inc(bvb_hi, 1)
            dve.wait_ge(bvb_hi, 1)
            nc.vector.tensor_tensor(BVB[:, 1], bvb, BVB[:, 0].bitcast(f32), ALU.subtract).then_inc(bvb_lo, 1)
            dve.wait_ge(lw_e, 1)
            nc.vector.tensor_scalar(lw[:, 2:3], lw[:, 1:2], 1.0, None, ALU.add).then_inc(lw_v, 1)
            dve.wait_ge(lw_v, 2)
            nc.vector.reciprocal(lw[:, 3:4], lw[:, 2:3]).then_inc(lw_v, 1)

            def lo_part(ready, count, dst, src, hi, done, bias=None):
                dve.wait_ge(ready, count)
                if bias is None:
                    nc.vector.tensor_tensor(dst, src, hi.bitcast(f32), ALU.subtract).then_inc(done, 1)
                else:
                    nc.vector.scalar_tensor_tensor(dst, src, bias, hi.bitcast(f32), ALU.add, ALU.subtract).then_inc(done, 1)

            for k in range(KD):
                lo_part(wvt_hi, k + 1, WVT[:, 1, k, :], bank(k), WVT[:, 0, k, :], wvt_lo)
            lo_part(gt_hi, 1, GWT[:, 1], bank(7)[:, 0:KD * NE].rearrange("p (k e) -> p k e", k=KD), GWT[:, 0], gt_lo)
            dve.wait_ge(crow_ps, 1)
            nc.vector.tensor_tensor(crow[:, :], bank(6), crow[:, :], ALU.add).then_inc(crow_ok, 1)

            for b in range(BATCH):
                for t in range(TB):
                    g = TB * b + t
                    lo_part(xt_hi, g + 1, XT[:, 1, :, t * P:(t + 1) * P], bank(g % 2).rearrange("p (k t) -> p k t", k=KD),
                            XT[:, 0, :, t * P:(t + 1) * P], xt_lo)
                for m in range(KD):
                    for h in range(NBB):
                        q = 16 * b + 2 * m + h
                        s = slice(h * BLK, (h + 1) * BLK)
                        lo_part(qk_hi, q + 1, KT[:, 1, m, s], bank(2 + q % 2), KT[:, 0, m, s], qk_lo,
                                bcol[:, KD + m:KD + m + 1])
                for c in range(2):
                    lo_part(vc_hi, 2 * b + c + 1, VC[:, 1, 4 * c:4 * c + 4, :],
                            bank(4 + c).rearrange("p (t d) -> p t d", t=4), VC[:, 0, 4 * c:4 * c + 4, :], vc_lo)
                for t in range(TB):
                    g = TB * b + t
                    lo_part(vw_hi, g + 1, VW[:, 1, t, :], bank(6 + g % 2), VW[:, 0, t, :], vw_lo)
                for m in range(KD):
                    for h in range(NBB):
                        q = 16 * b + 8 + 2 * m + h
                        s = slice(h * BLK, (h + 1) * BLK)
                        lo_part(qk_hi, q + 1, QT[:, 1, m, s], bank(2 + q % 2), QT[:, 0, m, s], qk_lo,
                                bcol[:, m:m + 1])
                for n in range(NBB):
                    B = NBB * b + n

                    def base_max(g):
                        dve.wait_ge(bs_ps, g + 1)
                        nc.vector.tensor_reduce(stat[:, 0, g:g + 1], bank(2 * (g % 2), 2), AX.X, ALU.max).then_inc(bs_mx, 1)
                        dve.wait_ge(bs_mx, g + 1)
                        nc.vector.tensor_scalar(stat[:, 1, g:g + 1], stat[:, 0, g:g + 1], -SCALE, None,
                                                ALU.mult).then_inc(bs_nm, 1)

                    def base_recip(g):
                        dve.wait_ge(bs_ex, g + 1)
                        nc.vector.reciprocal(stat[:, 3, g:g + 1], stat[:, 2, g:g + 1]).then_inc(bs_ri, 1)

                    for i in range(4):
                        base_max(4 * B + i)
                        if i:
                            base_recip(4 * B + i - 1)
                    base_recip(4 * B + 3)
                    for j in range(TB):
                        lo_part(bt_hi, TB * B + j + 1, PTB[j % 2][:, 1, :], bank(4 + j % 2), PTB[j % 2][:, 0, :], bt_lo)
                        if j == 0:
                            s = slice(n * BLK, (n + 1) * BLK)
                            dve.wait_ge(w_lo, WUNITS * (b + 1))
                            if n:
                                dve.wait_ge(qc_lo, B)
                            nc.vector.tensor_tensor(qfull, QT[:, 0, 0, s].bitcast(f32), QT[:, 1, 0, s].bitcast(f32),
                                                    ALU.add).then_inc(qf_ok, 1)
                    dve.wait_ge(tc_ok, B + 1)
                    dve.wait_ge(qf_ok, B + 1)
                    nc.vector.scalar_tensor_tensor(qfull, tcam, lw[:, 3:4], qfull, ALU.mult, ALU.add).then_inc(qn_ok, 1)
                    lo_part(qc_hi, B + 1, QT[:, 1, 0, s], qfull, QT[:, 0, 0, s], qc_lo)

                def final_max(g):
                    dve.wait_ge(fs_ps, g + 1)
                    nc.vector.tensor_reduce(stat[:, 4, g:g + 1], bank(0, 2), AX.X, ALU.max).then_inc(fs_mx, 1)
                    dve.wait_ge(fs_mx, g + 1)
                    nc.vector.tensor_scalar(stat[:, 5, g:g + 1], stat[:, 4, g:g + 1], -SCALE, None, ALU.mult).then_inc(fs_nm, 1)

                def residual(g):
                    dve.wait_ge(fo_mm, g + 1)
                    dve.wait_ge(xc_ok, TILES)
                    dve.wait_ge(fs_ri, g + 1)
                    nc.vector.scalar_tensor_tensor(acc[:, g, :], bank(4 + g % 2), stat[:, 7, g:g + 1], acc[:, g, :],
                                                   ALU.mult, ALU.add).then_inc(res_ok, 1)
                    dve.wait_ge(res_ok, g + 1)
                    nc.vector.bn_stats(bst[:, g, :], acc[:, g, :]).then_inc(bst_ok, 1)
                    dve.wait_ge(bst_ok, g + 1)
                    nc.vector.bn_aggr(bag[:, g, :], bst[:, g, :]).then_inc(bag_ok, 1)

                final_max(TB * b)
                for i in range(TB):
                    g = TB * b + i
                    for c in range(2):
                        lo_part(ft_hi, 2 * g + c + 1, PTF[g % 2][:, 1, 4 * c:4 * c + 4, :],
                                bank(2 + c).rearrange("p (t d) -> p t d", t=4), PTF[g % 2][:, 0, 4 * c:4 * c + 4, :], ft_lo)
                    dve.wait_ge(fs_ex, g + 1)
                    nc.vector.reciprocal(stat[:, 7, g:g + 1], stat[:, 6, g:g + 1]).then_inc(fs_ri, 1)
                    if i:
                        residual(g - 1)
                    if i < TB - 1:
                        final_max(g + 1)
                residual(TB * b + TB - 1)

            def norm_scale(n):
                dve.wait_ge(bag_ok, n * TILES)
                nc.vector.tensor_scalar(rstd[:, 0, :], bag[:, :, 1], EPS, None, ALU.add).then_inc(ve_ok, 1)
                dve.wait_ge(sq_ok, n)
                nc.vector.reciprocal(rstd[:, 2, :], rstd[:, 1, :]).then_inc(rs_ok, 1)
                dve.wait_ge(rs_ok, n)
                nc.vector.scalar_tensor_tensor(rstd[:, 0, :], bag[:, :, 0], -1.0, rstd[:, 2, :], ALU.mult,
                                               ALU.mult).then_inc(nm_ok, 1)
                dve.wait_ge(nm_ok, n)

            norm_scale(1)

            def norm_tile(t, done):
                return nc.vector.tensor_scalar(acc[:, t, :], acc[:, t, :], rstd[:, 2, t:t + 1], rstd[:, 0, t:t + 1],
                                               ALU.mult, ALU.add).then_inc(done, 1)

            norm_tile(0, x1_ok)
            norm_tile(1, x1_ok)
            for t in range(TILES):
                if t + 2 < TILES:
                    norm_tile(t + 2, x1_ok)
                lo_part(x1t_hi, t + 1, X1T[:, 1, :, t * P:(t + 1) * P], bank(t % 4).rearrange("p (k t) -> p k t", k=KD),
                        X1T[:, 0, :, t * P:(t + 1) * P], x1t_lo)

            steps = [0]

            def link(ins):
                steps[0] += 1
                ins.then_inc(rt_step, 1)
                dve.wait_ge(rt_step, steps[0])

            def rank_tiles(q):
                s4 = sc[:, 4 * q:4 * q + 4, :]
                other = s4.unsqueeze(2).to_broadcast([P, 4, NE, NE])
                own = s4.unsqueeze(3).to_broadcast([P, 4, NE, NE])
                if q == 0:
                    dve.wait_ge(lg_sg, 1)
                    dve.wait_ge(below_ok, 2)
                    link(nc.vector.tensor_tensor(sc, sc, gb[:, :].unsqueeze(1).to_broadcast([P, TILES, NE]), ALU.add))
                link(nc.vector.tensor_tensor(cmp_a, other, own, ALU.is_equal))
                link(nc.vector.tensor_tensor(cmp_a, cmp_a, below.unsqueeze(1).to_broadcast([P, 4, NE, NE]), ALU.mult))
                link(nc.vector.tensor_tensor(cmp_b, other, own, ALU.is_gt))
                link(nc.vector.tensor_tensor(cmp_a, cmp_a, cmp_b, ALU.add))
                link(nc.vector.tensor_reduce(rk[:, 4 * q:4 * q + 4, :], cmp_a, AX.X, ALU.add))

            def router_weights():
                link(nc.vector.tensor_scalar(rk, rk, float(TOPK), None, ALU.is_lt))
                link(nc.vector.tensor_tensor(pr, sc, rk, ALU.mult))
                link(nc.vector.tensor_reduce(wsum, pr, AX.X, ALU.add))
                link(nc.vector.reciprocal(winv, wsum))
                nc.vector.tensor_tensor(pr, pr, winv.unsqueeze(2).to_broadcast([P, TILES, NE]), ALU.mult).then_inc(pr_ok, 1)

            def evacuate(nb, before, units):
                dve.wait_ge(o_mm, units)
                if before is not None:
                    dve.wait_ge(acc_ok, before)
                for s in range(TPB):
                    t = nb * TPB + s
                    last = nc.vector.tensor_tensor(acc[:, t, :], bank(4 + s), acc[:, t, :], ALU.add)
                last.then_inc(acc_ok, 1)

            for u in range(SHU):
                nb, c = divmod(u, SHC)
                dve.wait_ge(h1_cp, u + 1)
                nc.vector.tensor_tensor(ub[:, u % 4, :], ub[:, u % 4, :], bank(2 * (u % 2) + 1), ALU.mult).then_inc(h3_ok, 1)
                lo_part(hb_hi, u + 1, HB[u % 2][:, 1, :], ub[:, u % 4, :], HB[u % 2][:, 0, :], hb_lo)
                if c == 0 and nb:
                    evacuate(nb - 1, nb - 1 if nb > 1 else None, u)
                if u in (1, 2, 4, 5):
                    rank_tiles((1, 2, 4, 5).index(u))
                if u == 6:
                    router_weights()

            BPI = len(GROUPS) * NBLK
            with nc.vector.Fori(0, ITERS) as it:
                for gi, (first, slots) in enumerate(GROUPS):
                    size = len(slots)
                    for nb in range(NBLK):
                        for c in range(size):
                            k = first * NBLK + nb * size + c
                            u = it * ITU + (SHU + k)
                            kr = it * ITU + (k + 1)
                            dve.wait_ge(h1_cp, u + 1)
                            nc.vector.tensor_tensor(ub[:, k % 4, :], ub[:, k % 4, :], bank(2 * (k % 2) + 1),
                                                    ALU.mult).then_inc(z_ok, 1)
                            dve.wait_ge(silu_ok, kr)
                            npb = sum(len(pieces(f + cc)) for f, ss in GROUPS for n2 in range(NBLK)
                                      for cc in range(len(ss))
                                      if (f * NBLK + n2 * len(ss) + cc) % 4 == k % 4 and f * NBLK + n2 * len(ss) + cc <= k)
                            tot = sum(len(pieces(f + cc)) for f, ss in GROUPS for n2 in range(NBLK)
                                      for cc in range(len(ss)) if (f * NBLK + n2 * len(ss) + cc) % 4 == k % 4)
                            dve.wait_ge(pb_ld[k % 4], it * (16 * tot) + 16 * npb)
                            nc.vector.tensor_tensor(ub[:, k % 4, :], ub[:, k % 4, :], pb[:, k % 4, :], ALU.mult).then_inc(h3_ok, 1)
                            lo_part(hb_hi, u + 1, HB[k % 2][:, 1, :], ub[:, k % 4, :], HB[k % 2][:, 0, :], hb_lo)
                            if c == 0:
                                evacuate((nb - 1) % NBLK, it * BPI + (NBLK + gi * NBLK + nb - 1), u)
            evacuate(NBLK - 1, ITERS * BPI + NBLK - 1, SHU + ITERS * ITU)
            dve.wait_ge(acc_ok, ITERS * BPI + NBLK)

            for t in range(TILES):
                nc.vector.bn_stats(bst[:, t, :], acc[:, t, :]).then_inc(bst_ok, 1)
                if t:
                    dve.wait_ge(bst_ok, TILES + t)
                    nc.vector.bn_aggr(bag[:, t - 1, :], bst[:, t - 1, :]).then_inc(bag_ok, 1)
            dve.wait_ge(bst_ok, 2 * TILES)
            nc.vector.bn_aggr(bag[:, TILES - 1, :], bst[:, TILES - 1, :]).then_inc(bag_ok, 1)
            norm_scale(2)
            for t in range(TILES):
                norm_tile(t, out_ok)

        @block.tensor
        def _(pe):
            def product(dst, lhs, rhs, first, last):
                ts = terms(lhs, rhs)
                for i, (a, b_) in enumerate(ts):
                    ins = nc.tensor.matmul(dst, a, b_, start=first and i == 0, stop=last and i == 2)
                return ins

            pe.wait_ge(id_step, 2)
            pe.wait_ge(const_ld, 16 * (SMALL - 1))
            for k in range(KD):
                ins = nc.tensor.transpose(bank(7)[:, k * NE:(k + 1) * NE], gw[:, k * P:(k + 1) * P], ident[0:NE, 0:NE])
            ins.then_inc(gt_ps, 1)
            for ke in range(KD):
                for kd in range(KD):
                    ins = nc.tensor.transpose(bank(ke)[:, kd * P:(kd + 1) * P], wv_raw[:, kd, ke * P:(ke + 1) * P], ident[:, :])
                ins.then_inc(wvt_ps, 1)
            pe.wait_ge(wvt_lo, KD)
            pe.wait_ge(wp_lo, 1)
            for kd in range(KD):
                if kd >= 2:
                    pe.wait_ge(wvp_cp, kd - 1)
                for ke in range(KD):
                    ins = product(bank(4 + kd % 2), lambda i: WVT[:, i, ke, kd * P:(kd + 1) * P], lambda i: WPR[:, i, ke, :],
                                  ke == 0, ke == KD - 1)
                ins.then_inc(wvp_ps, 1)
            pe.wait_ge(bvb_lo, 1)
            for ke in range(KD):
                ins = product(bank(6), lambda i: BVB[:, i, ke, :], lambda i: WPR[:, i, ke, :], ke == 0, ke == KD - 1)
            ins.then_inc(crow_ps, 1)

            for b in range(BATCH):
                for t in range(TB):
                    g = TB * b + t
                    pe.wait_ge(xst_ld[g % 2], 16 * (g // 2 + 1))
                    if g >= 2:
                        pe.wait_ge(xt_lo, g - 1)
                    if b and t == 0:
                        pe.wait_ge(fs_ex, g)
                    for k in range(KD):
                        ins = nc.tensor.transpose(bank(g % 2)[:, k * P:(k + 1) * P], xst[:, g % 2, k * P:(k + 1) * P],
                                                  ident[:, :])
                    ins.then_inc(xt_ps, 1)

                def project(q, m, h, unit):
                    pe.wait_ge(w_lo, unit + 1)
                    pe.wait_ge(xt_lo, TB * b + 4 * (h + 1))
                    if q >= 2:
                        pe.wait_ge(qk_lo, q - 1)
                    return q

                for m in range(KD):
                    for h in range(NBB):
                        q = project(16 * b + 2 * m + h, m, h, unit_k(b, m))
                        ws = WS[ring_no(b, m) % 2]
                        for k in range(KD):
                            ins = product(bank(2 + q % 2), lambda i: ws[:, i, k, :],
                                          lambda i: XT[:, i, k, h * BLK:(h + 1) * BLK], k == 0, k == KD - 1)
                        ins.then_inc(qk_ps, 1)
                pe.wait_ge(w_lo, unit_vc(b) + 1)
                ws = WS[ring_no(b, KD) % 2]
                for t in range(TB):
                    for k in range(KD):
                        ins = product(bank(4 + t // 4)[:, (t % 4) * P:(t % 4 + 1) * P],
                                      lambda i: XT[:, i, k, t * P:(t + 1) * P], lambda i: ws[:, i, k, :], k == 0, k == KD - 1)
                    if t % 4 == 3:
                        ins.then_inc(vc_ps, 1)
                pe.wait_ge(w_lo, unit_wvp(b, KD - 1) + 1)
                for t in range(TB):
                    g = TB * b + t
                    if g >= 2:
                        pe.wait_ge(vw_lo, g - 1)
                    if g == 0:
                        pe.wait_ge(crow_ok, 1)
                        pe.wait_ge(gt_lo, 1)
                    for k in range(KD):
                        ins = product(bank(6 + g % 2), lambda i: XT[:, i, k, t * P:(t + 1) * P], lambda i: WVP[:, i, k, :],
                                      k == 0, k == KD - 1)
                    ins.then_inc(vw_ps, 1)
                for m in range(KD):
                    for h in range(NBB):
                        q = project(16 * b + 8 + 2 * m + h, m, h, unit_q(b, m))
                        ws = WS[ring_no(b, KD + 1 + m) % 2]
                        for k in range(KD):
                            ins = product(bank(2 + q % 2), lambda i: ws[:, i, k, :],
                                          lambda i: XT[:, i, k, h * BLK:(h + 1) * BLK], k == 0, k == KD - 1)
                        ins.then_inc(qk_ps, 1)

                pe.wait_ge(qk_lo, 16 * (b + 1))
                pe.wait_ge(vc_lo, 2 * (b + 1))
                pe.wait_ge(vw_lo, TB * (b + 1))
                for n in range(NBB):
                    B = NBB * b + n
                    for i in range(4):
                        g = 4 * B + i
                        t = 4 * n + i
                        if g >= 2:
                            pe.wait_ge(bs_ex, g - 1)
                        for h in range(2):
                            ins = product(bank(2 * (g % 2) + h), lambda p_: QT[:, p_, 0, t * P:(t + 1) * P],
                                          lambda p_: KT[:, p_, 0, h * BLK:(h + 1) * BLK], True, True)
                        ins.then_inc(bs_ps, 1)

                    def transpose_base(j):
                        k = TB * B + j
                        if k >= 2:
                            pe.wait_ge(bt_lo, k - 1)
                        for i in range(4):
                            pe.wait_ge(bs_no, 4 * B + i + 1)
                            ins = nc.tensor.transpose(bank(4 + j % 2)[:, i * P:(i + 1) * P], probs[:, i, j * P:(j + 1) * P],
                                                      ident[:, :])
                        ins.then_inc(bt_ps, 1)

                    transpose_base(0)
                    for j in range(TB):
                        if j + 1 < TB:
                            transpose_base(j + 1)
                        pe.wait_ge(bt_lo, TB * B + j + 1)
                        if j == 0 and B:
                            pe.wait_ge(tc_ok, B)
                        product(bank(6), lambda p_: VC[:, p_, j, :], lambda p_: PTB[j % 2][:, p_, :],
                                j == 0, j == TB - 1).then_inc(bc_mm, 1)

                def scores(g):
                    t = g % TB
                    if t == 0:
                        pe.wait_ge(bs_ex, TB * (b + 1))
                    pe.wait_ge(qc_lo, NBB * b + t // 4 + 1)
                    if t:
                        pe.wait_ge(fs_ex, g)
                    for h in range(2):
                        for k in range(KD):
                            ins = product(bank(h), lambda p_: QT[:, p_, k, t * P:(t + 1) * P],
                                          lambda p_: KT[:, p_, k, h * BLK:(h + 1) * BLK], k == 0, k == KD - 1)
                    ins.then_inc(fs_ps, 1)

                scores(TB * b)
                for i in range(TB):
                    g = TB * b + i
                    pe.wait_ge(fs_ex, g + 1)
                    for c in range(2):
                        if i:
                            pe.wait_ge(ft_lo, 2 * (g - 1) + c + 1)
                        for j in range(4):
                            tj = 4 * c + j
                            ins = nc.tensor.transpose(bank(2 + c)[:, j * P:(j + 1) * P],
                                                      probs[:, i % 4, tj * P:(tj + 1) * P], ident[:, :])
                        ins.then_inc(ft_ps, 1)
                    if i + 1 < TB:
                        scores(g + 1)
                    if g >= 2:
                        pe.wait_ge(res_ok, g - 1)
                    for j in range(TB):
                        if j % 4 == 0:
                            pe.wait_ge(ft_lo, 2 * g + j // 4 + 1)
                        ins = product(bank(4 + g % 2), lambda p_: PTF[g % 2][:, p_, j, :], lambda p_: VW[:, p_, j, :],
                                      j == 0, j == TB - 1)
                    ins.then_inc(fo_mm, 1)

            for t in range(TILES):
                pe.wait_ge(x1_ok, t + 1)
                if t >= 4:
                    pe.wait_ge(x1t_lo, t - 3)
                for k in range(KD):
                    ins = nc.tensor.transpose(bank(t % 4)[:, k * P:(k + 1) * P], acc[:, t, k * P:(k + 1) * P], ident[:, :])
                ins.then_inc(x1t_ps, 1)
            pe.wait_ge(gt_lo, 1)
            pe.wait_ge(res_ok, TILES)
            for t in range(TILES):
                pe.wait_ge(x1t_lo, t + 1)
                for k in range(KD):
                    ins = product(bank(4)[:, t * NE:(t + 1) * NE], lambda i: X1T[:, i, k, t * P:(t + 1) * P],
                                  lambda i: GWT[:, i, k, :], k == 0, k == KD - 1)
            ins.then_inc(lg_ps, 1)

            def hidden(slot, nb, par):
                for w, bk in ((W1, 2 * par), (W3, 2 * par + 1)):
                    for k in range(KD):
                        ins = product(bank(bk), lambda i: w[slot][:, i, k, :],
                                      lambda i: X1T[:, i, k, nb * BLK:(nb + 1) * BLK], k == 0, k == KD - 1)
                ins.then_inc(h_mm, 1)

            def down(slot, par, first, last):
                for s in range(TPB):
                    ins = product(bank(4 + s), lambda i: HB[par][:, i, s * P:(s + 1) * P], lambda i: W2[slot][:, i, :],
                                  first, last)
                ins.then_inc(o_mm, 1)

            for u in range(SHU):
                nb, c = divmod(u, SHC)
                if nb == 0:
                    pe.wait_ge(fw_lo, 3 * c + 3)
                if u >= 8:
                    rb = 2 * ((u - 8 + 1) % 2)
                    pe.wait_ge(hb_lo, u)
                    pe.wait_ge(pr_ok, 1)
                    if u - 8 >= 2:
                        pe.wait_ge(pt_cp, u - 9)
                    for s in range(TPB):
                        ins = nc.tensor.transpose(bank(rb)[0:NE, s * P:(s + 1) * P], pr[:, 4 * (u - 8) + s, :], ident[:, :])
                    ins.then_inc(pt_ps, 1)
                    if u - 8 >= 1:
                        pe.wait_ge(pt_cp, u - 8)
                hidden(SH_SLOTS[c], nb, u % 2)
                if u:
                    pnb, pc = divmod(u - 1, SHC)
                    pe.wait_ge(hb_lo, u)
                    if u == 1:
                        pe.wait_ge(lg_sg, 1)
                    if pc == 0 and pnb:
                        pe.wait_ge(acc_ok, pnb)
                    down(SH_SLOTS[pc], (u - 1) % 2, pc == 0, pc == SHC - 1)

            BPI = len(GROUPS) * NBLK
            order = [(gi, first, slots, nb, c) for gi, (first, slots) in enumerate(GROUPS)
                     for nb in range(NBLK) for c in range(len(slots))]

            def down_routed(k, units, blocks):
                gi, first, slots, nb, c = order[k]
                pe.wait_ge(hb_lo, units)
                if c == 0:
                    pe.wait_ge(acc_ok, blocks)
                down(slots[c], k % 2, c == 0, c == len(slots) - 1)

            pe.wait_ge(pt_cp, NBLK)
            with nc.tensor.Fori(0, ITERS) as it:
                for k, (gi, first, slots, nb, c) in enumerate(order):
                    if nb == 0:
                        pe.wait_ge(fw_lo, it * (3 * CH) + 3 * (SHC + first + c + 1))
                    hidden(slots[c], nb, k % 2)
                    if k == 0:
                        pe.wait_ge(hb_lo, it * ITU + SHU)
                        down(GROUPS[-1][1][-1], 1, False, True)
                    else:
                        pgi, _, _, pnb, _ = order[k - 1]
                        down_routed(k - 1, it * ITU + (SHU + k), it * BPI + (NBLK + pgi * NBLK + pnb))
            pe.wait_ge(hb_lo, SHU + ITERS * ITU)
            down(GROUPS[-1][1][-1], 1, False, True)


_INS = ['L0_attn_hidden_states', 'L0_attn_c_attn_w', 'L0_attn_c_attn_b', 'L0_attn_c_proj_w', 'L0_attn_c_proj_b',
        'L0_attn_cam_gate', 'L0_attn_cam_w0', 'L0_attn_cam_w1', 'L0_ffn_gate_w', 'L0_ffn_gate_b',
        'L0_ffn_w1_shared', 'L0_ffn_w2_shared', 'L0_ffn_w3_shared', 'L0_ffn_w1_routed', 'L0_ffn_w2_routed',
        'L0_ffn_w3_routed']


def kernel(**inputs):
    import numpy as _np
    import concourse.bacc as _bacc
    from concourse import mybir as _mybir
    from concourse.bass_utils import run_bass_kernel_spmd as _run

    nc = _bacc.Bacc("TRN2", target_bir_lowering=False, num_devices=1)
    arrays, args = {}, []
    for name in _INS:
        a = _np.ascontiguousarray(inputs[name])
        arrays[f"in_{name}_dram"] = a
        args.append(nc.dram_tensor(f"in_{name}_dram", a.shape, _mybir.dt.from_np(a.dtype), kind="ExternalInput").ap())
    fp32 = _mybir.dt.float32
    x_shape = inputs['L0_attn_hidden_states'].shape
    tokens = x_shape[0] * x_shape[1]
    width = x_shape[2]
    experts = inputs['L0_ffn_gate_w'].shape[0]
    args.append(nc.dram_tensor("router_weights_dram", (experts, tokens), fp32, kind="Internal").ap())
    args.append(nc.dram_tensor("value_projection_dram", (width, width), fp32, kind="Internal").ap())
    args.append(nc.dram_tensor("out_0_dram", x_shape, fp32, kind="ExternalOutput").ap())
    post_ln_attention_moe_kernel(nc, *args)
    r = _run(nc, [arrays], core_ids=[0])
    return r.results[0]["out_0_dram"]
```

```python
import concourse.bass as bass
from concourse import mybir
from contextlib import ExitStack



def post_ln_attention_moe_kernel(
    nc, hidden_states, c_attn_w, c_attn_b, c_proj_w, c_proj_b, cam_gate, cam_w0, cam_w1,
    gate_w, gate_b, w1_shared, w2_shared, w3_shared, w1_routed, w2_routed, w3_routed,
    router_dram, vproj_dram, out,
):
    f32 = mybir.dt.float32
    f32r = mybir.dt.float32r
    ALU = mybir.AluOpType
    ACT = mybir.ActivationFunctionType
    AX = mybir.AxisListType

    P = 128
    BATCH, SEQ, D = hidden_states.shape
    KD = D // P
    TB = SEQ // P
    TILES = BATCH * TB
    BLK = 512
    TPB = BLK // P
    NBB = SEQ // BLK
    NBLK = BATCH * NBB
    DCAM = cam_gate.shape[0]
    SCALE = 1.0 / float(32) ** 0.5
    NE, _, HID = w1_routed.shape
    HSH = w1_shared.shape[1]
    TOPK = 4
    EPS = 1e-5
    assert DCAM == P

    SB = 4
    CH = SB * HID // P
    ITERS = NE // SB
    GROUPS = [(0, [0, 1]), (2, [3, 4, 5]), (5, [0, 1, 2]), (8, [3, 4, 5])]
    NSLOT = 6
    SHC = -(-HSH // P)
    SH_SLOTS = [3, 4, 5]
    SHU = SHC * NBLK
    ITU = CH * NBLK

    def pieces(j):
        res, r = [], 0
        while r < P:
            e, c = divmod(P * j + r, HID)
            n = min(P - r, HID - c)
            res.append((e, c, r, n))
            r += n
        return res

    x_tiles = hidden_states.rearrange("b (t p) d -> (b t) p d", p=P)
    out_tiles = out.rearrange("b (t p) d -> (b t) p d", p=P)
    wqkv = c_attn_w.rearrange("(k p) n -> p k n", p=P)
    bqkv = c_attn_b.rearrange("(m p) -> p m", p=P)
    wp_v = c_proj_w.rearrange("(k p) n -> p k n", p=P)
    w1s = w1_shared.rearrange("(k p) h -> p k h", p=P)
    w3s = w3_shared.rearrange("(k p) h -> p k h", p=P)
    w1r = w1_routed.rearrange("e (k p) h -> e p k h", p=P)
    w3r = w3_routed.rearrange("e (k p) h -> e p k h", p=P)
    w2r = w2_routed.rearrange("e h d -> (e h) d")

    ctx = ExitStack()
    with ctx:
        def sb(name, shape, dt=f32):
            return ctx.enter_context(nc.sbuf_tensor(name, shape, dt))

        def sem(name):
            return ctx.enter_context(nc.semaphore(name))

        ps = ctx.enter_context(nc.psum_tensor("ps", [P, 8 * BLK], f32))

        def bank(i, n=1):
            return ps[:, i * BLK:(i + n) * BLK]

        R = sb("R", [P, 38 * 1024], f32r)
        acc = sb("acc", [P, TILES, D])
        scratch = sb("scratch", [P, 4 * BLK])
        raw = sb("raw", [P, 3, BLK])
        small = sb("small", [P, 2, BLK])
        crow = sb("crow", [P, D])
        GWT = sb("GWT", [P, 2, KD, NE], f32r)
        ident = sb("ident", [P, P])
        bcol = sb("bcol", [P, 3 * KD])
        gcol = sb("gcol", [P, 1])
        gbv = sb("gbv", [P, 1])
        w0c = sb("w0c", [P, 1])
        w1c = sb("w1c", [P, 1])
        lw = sb("lw", [P, 4])
        ones = sb("ones", [P, 1])
        stat = sb("stat", [P, 8, TILES])
        bst = sb("bst", [P, TILES, 6])
        bag = sb("bag", [P, TILES, 2])
        rstd = sb("rstd", [P, 3, TILES])
        gb = sb("gb", [P, NE])

        def view(off, *dims):
            n = 1
            for d in dims:
                n *= d
            v = R[:, off:off + n]
            if len(dims) == 2:
                return v.rearrange("p (a b) -> p a b", a=dims[0])
            return v.rearrange("p (a b c) -> p a b c", a=dims[0], b=dims[1])

        XT = view(0, 2, KD, SEQ)
        KT = view(8192, 2, KD, SEQ)
        QT = view(16384, 2, KD, SEQ)
        WVP = [R[:, 16384 + (1 + KD * i) * SEQ:16384 + (1 + KD * i) * SEQ + KD * D].rearrange("p (k n) -> p k n", k=KD)
               for i in range(2)]
        VW = view(24576, 2, TB, D)
        VC = view(32768, 2, TB, DCAM)
        PTF = view(32768, 2, TB, P)
        WS = [view(34816 + 1024 * s, 2, KD, P) for s in range(2)]
        PTB = [view(36864 + 1024 * s, 2, BLK) for s in range(2)]
        WVT = view(24576, 2, KD, D)
        WPR = view(28672, 2, KD, D)
        BVB = view(36864, 2, KD, P)
        X1T = [view(8192 * b, 2, KD, SEQ) for b in range(BATCH)]
        slot_at = [16384 + 3072 * ((s + 3) % NSLOT) for s in range(NSLOT)]
        W1 = [view(a, 2, KD, P) for a in slot_at]
        W3 = [view(a + 1024, 2, KD, P) for a in slot_at]
        W2 = [view(a + 2048, 2, D) for a in slot_at]
        HB = [view(34816 + 1024 * s, 2, BLK) for s in range(2)]
        pb = R[:, 36864:36864 + 4 * BLK].rearrange("p (s t) -> p s t", s=4).bitcast(f32)
        cmp_a_w = R[:, 36864:37888].rearrange("p (t e j) -> p t e j", t=TPB, e=NE)
        cmp_b_w = R[:, 37888:38912].rearrange("p (t e j) -> p t e j", t=TPB, e=NE)
        cmp_a, cmp_b = cmp_a_w.bitcast(f32), cmp_b_w.bitcast(f32)

        upper = acc[:, TB:2 * TB, :]
        base_p = upper.rearrange("p (s h) d -> p s (h d)", s=4)
        wv_raw = acc[:, TB:TB + KD, :]
        wp_raw = acc[:, TB + KD:TB + 2 * KD, :]
        final_p = scratch[:, :].rearrange("p (s t) -> p s t", s=2)
        tcam, qfull = scratch[:, 2 * BLK:3 * BLK], scratch[:, 3 * BLK:4 * BLK]
        gw = scratch[0:NE, 0:D]
        ub = scratch[:, :].rearrange("p (s t) -> p s t", s=4)
        sc = small[:, 0, 0:256].rearrange("p (t e) -> p t e", t=TILES)
        rk = small[:, 0, 256:512].rearrange("p (t e) -> p t e", t=TILES)
        pr = small[:, 1, 0:256].rearrange("p (t e) -> p t e", t=TILES)
        below = small[:, 1, 256:512].rearrange("p (e j) -> p e j", e=NE)
        prT = small[0:NE, 0, :]
        wsum = stat[:, 0, :]
        winv = stat[:, 1, :]

        bias_ld, const_ld, wvwp_ld = sem("bias_ld"), sem("const_ld"), sem("wvwp_ld")
        x_ld = [sem(f"x_ld{t}") for t in range(TB)]
        raw_ld = [sem(f"raw_ld{s}") for s in range(3)]
        id_step = sem("id_step")
        wp_hi, wp_lo = sem("wp_hi"), sem("wp_lo")
        w_hi, w_lo = sem("w_hi"), sem("w_lo")
        wvt_ps, wvt_hi, wvt_lo = sem("wvt_ps"), sem("wvt_hi"), sem("wvt_lo")
        bvb_hi, bvb_lo = sem("bvb_hi"), sem("bvb_lo")
        wvp_ps, wvp_hi, wvp_lo = sem("wvp_ps"), sem("wvp_hi"), sem("wvp_lo")
        wvp_st, wvp_ld = sem("wvp_st"), sem("wvp_ld")
        crow_ps, crow_ok = sem("crow_ps"), sem("crow_ok")
        lw_v, lw_e = sem("lw_v"), sem("lw_e")
        gbv_ok = sem("gbv_ok")
        xt_ps, xt_hi, xt_lo = sem("xt_ps"), sem("xt_hi"), sem("xt_lo")
        pj_ps, pj_hi, pj_lo = sem("pj_ps"), sem("pj_hi"), sem("pj_lo")
        vc_ps, vc_hi, vc_lo = sem("vc_ps"), sem("vc_hi"), sem("vc_lo")
        bs_ps, bs_mx, bs_nm, bs_ex, bs_ri, bs_no = (sem(f"bs_{n}") for n in ("ps", "mx", "nm", "ex", "ri", "no"))
        bt_ps, bt_hi, bt_lo, bc_mm = sem("bt_ps"), sem("bt_hi"), sem("bt_lo"), sem("bc_mm")
        tc_ok, qf_ok, qn_ok, qc_hi, qc_lo = sem("tc_ok"), sem("qf_ok"), sem("qn_ok"), sem("qc_hi"), sem("qc_lo")
        fs_ps, fs_mx, fs_nm, fs_ex, fs_ri = (sem(f"fs_{n}") for n in ("ps", "mx", "nm", "ex", "ri"))
        ft_ps, ft_hi, ft_lo, fo_mm = sem("ft_ps"), sem("ft_hi"), sem("ft_lo"), sem("fo_mm")
        xc_ok, res_ok, bst_ok, bag_ok = sem("xc_ok"), sem("res_ok"), sem("bst_ok"), sem("bag_ok")
        ve_ok, sq_ok, rs_ok, nm_ok, x1_ok = sem("ve_ok"), sem("sq_ok"), sem("rs_ok"), sem("nm_ok"), sem("x1_ok")
        gt_ps, gt_hi, gt_lo = sem("gt_ps"), sem("gt_hi"), sem("gt_lo")
        lg_ps, lg_cp, lt_ps, lg_sg = sem("lg_ps"), sem("lg_cp"), sem("lt_ps"), sem("lg_sg")
        rt_step, below_ok, pr_ok, pt_ps, pt_cp, pt_st = (sem(n) for n in ("rt_step", "below_ok", "pr_ok", "pt_ps", "pt_cp", "pt_st"))
        wraw_ld = [sem(f"wraw_ld{s}") for s in range(3)]
        pad_ok = sem("pad_ok")
        fw_hi, fw_lo = sem("fw_hi"), sem("fw_lo")
        pb_ld = [sem(f"pb_ld{s}") for s in range(4)]
        h_mm, h1_cp, z_ok, silu_ok, h3_ok, hb_hi, hb_lo, o_mm, acc_ok = (
            sem(n) for n in ("h_mm", "h1_cp", "z_ok", "silu_ok", "h3_ok", "hb_hi", "hb_lo", "o_mm", "acc_ok"))
        last_mm, last_ok = sem("last_mm"), sem("last_ok")
        out_ok, out2_ok, out_st = sem("out_ok"), sem("out2_ok"), sem("out_st")

        HEAD = [("K", 0, 0), ("Q", 0, 0), ("K", 0, 1), ("Q", 0, 1), ("C", 0, 0), ("C", 0, 1)]
        FILL = ([("K", m, h) for m in range(1, KD) for h in range(NBB)] + [("V", t, 0) for t in range(TB)]
                + [("Q", m, h) for m in range(1, KD) for h in range(NBB)])
        JOBS = HEAD + FILL
        NJ = len(JOBS)
        CAM = []
        fill = len(HEAD)
        for n in range(NBB):
            for i in range(TPB):
                CAM += [("S", n, i), ("f", n, fill), ("F", n, fill)]
                fill += 1
                if n == 0 and i < 2:
                    CAM.append(("V", n, i))
            CAM += [("f", n, fill), ("F", n, fill), ("T", n, 0), ("f", n, fill + 1), ("F", n, fill + 1)]
            fill += 2
            for j in range(TB):
                if j + 1 < TB:
                    CAM.append(("T", n, j + 1))
                CAM += [("C", n, j), ("fF"[j % 2], n, fill)]
                fill += j % 2
        assert fill == NJ
        WORDER = [("K", 0), ("Q", 0), ("C", 0)] + [("K", m) for m in range(1, KD)] + [("Q", m) for m in range(1, KD)]
        NW = len(WORDER)
        assert NW % 3 == 0

        def weight_no(b, kind, m):
            return NW * b + WORDER.index((kind, m))

        VCT = small[:, :, :].rearrange("p a n -> p (a n)")

        def job_dst(kind, m, h):
            s = slice(h * BLK, (h + 1) * BLK)
            if kind == "K":
                return KT[:, 0, m, s], KT[:, 1, m, s], bcol[:, KD + m:KD + m + 1]
            if kind == "Q":
                return QT[:, 0, m, s], QT[:, 1, m, s], bcol[:, m:m + 1]
            return VW[:, 0, m, :], VW[:, 1, m, :], None

        def tiled(ap):
            return ap.rearrange("p (k t) -> p k t", k=KD)

        def xt_dst(n):
            b, t = divmod(n, TB)
            v = XT if b < BATCH else X1T[b - BATCH]
            return [v[:, i, :, t * P:(t + 1) * P] for i in range(2)]

        def xt_bank(n):
            return 6 + n % 2 if n < 3 * TB else 4 + n % 2

        def score_banks(i):
            return bank(4, 2) if i == 1 else bank(0, 2)

        def shared_rows(c):
            return min(P, HSH - c * P)

        PT_U = 8
        RANK_U = (1, 2, 4, 5)
        BPI = len(GROUPS) * NBLK
        ORDER = [(gi, first + c, slots[c], nb, c == 0, c == len(slots) - 1)
                 for gi, (first, slots) in enumerate(GROUPS) for nb in range(NBLK) for c in range(len(slots))]
        PB_DMAS = [sum(len(pieces(ORDER[i][1])) for i in range(k % 4, k + 1, 4)) for k in range(ITU)]
        PB_ALL = [sum(len(pieces(ORDER[i][1])) for i in range(s, ITU, 4)) for s in range(4)]

        block = ctx.enter_context(nc.Block())

        @block.sync
        def _(sp):
            def load_x(b, t):
                sp.dma_start(acc[:, TB * b + t, :], x_tiles[TB * b + t]).then_inc(x_ld[t], 16)

            def load_raw(n):
                kind, m = WORDER[n % NW]
                col = {"Q": 0, "K": D, "C": 2 * D}[kind] + m * P
                if n >= 3:
                    sp.wait_ge(w_lo, n - 2)
                sp.dma_start(tiled(raw[:, n % 3, :]), wqkv[:, :, col:col + P]).then_inc(raw_ld[n % 3], 16)

            for t in range(TPB):
                load_x(0, t)
            load_raw(0)
            sp.dma_start(bcol[:, :], bqkv, allow_slow_non_contiguous=True).then_inc(bias_ld, 16)
            load_raw(1)
            for t in range(TPB, TB):
                load_x(0, t)
            load_raw(2)
            sp.dma_start(wv_raw, wqkv[:, :, 2 * D:3 * D]).then_inc(wvwp_ld, 16)
            sp.dma_start(wp_raw, wp_v).then_inc(wvwp_ld, 16)
            sp.dma_start(gw, gate_w).then_inc(const_ld, 16)
            sp.dma_start(gcol[:, :], cam_gate.rearrange("(p a) -> p a", a=1)).then_inc(const_ld, 16)
            sp.dma_start(w0c[:, :], cam_w0.rearrange("(a n) -> a n", a=1).to_broadcast([P, 1])).then_inc(const_ld, 16)
            sp.dma_start(w1c[:, :], cam_w1.rearrange("(a n) -> a n", a=1).to_broadcast([P, 1])).then_inc(const_ld, 16)
            sp.dma_start(crow[:, :], c_proj_b.rearrange("(a n) -> a n", a=1).to_broadcast([P, D])).then_inc(const_ld, 16)
            sp.dma_start(gb[:, :], gate_b.rearrange("(a n) -> a n", a=1).to_broadcast([P, NE])).then_inc(const_ld, 16)
            load_raw(3)
            load_raw(4)
            sp.wait_ge(wvp_lo, KD)
            for i in range(2):
                sp.dma_start(vproj_dram[i], WVP[i].bitcast(f32)).then_inc(wvp_st, 16)
            for n in range(5, NW):
                load_raw(n)
            sp.wait_ge(bt_ps, TB * NBB)
            for t in range(TB):
                load_x(1, t)
            for n in range(NW, NW + 3):
                load_raw(n)
            sp.wait_ge(fs_ps, TB)
            sp.wait_ge(wvp_st, 32)
            for i in range(2):
                sp.dma_start(WVP[i].bitcast(f32), vproj_dram[i]).then_inc(wvp_ld, 16)
            for n in range(NW + 3, 2 * NW):
                load_raw(n)
            sp.wait_ge(bt_ps, 2 * TB * NBB)
            for t in range(TB):
                load_x(1, t)

            for c in range(SHC):
                n = shared_rows(c)
                for kind, wsrc in ((0, w1s), (1, w3s)):
                    sp.wait_ge(*((fw_lo, 3 * c + kind - 2) if c else (w_lo, 2 * NW)))
                    sp.dma_start(tiled(raw[:, kind, :])[:, :, 0:n], wsrc[:, :, c * P:c * P + n]).then_inc(wraw_ld[kind], 16)
                if c:
                    sp.wait_ge(fw_lo, 3 * c)
                sp.dma_start(raw[0:n, 2, :], w2_shared[c * P:c * P + n, :]).then_inc(wraw_ld[2], 16)

            with nc.sync.Fori(0, ITERS) as it:
                for j in range(CH):
                    free = it * (3 * CH) + 3 * (SHC + j)
                    for kind, wsrc in ((0, w1r), (1, w3r)):
                        sp.wait_ge(fw_lo, free + (kind - 2))
                        for e, c, r, n in pieces(j):
                            sp.dma_start(tiled(raw[:, kind, :])[:, :, r:r + n],
                                         wsrc[bass.ds(it * SB + e, 1), :, :, c:c + n].rearrange(
                                             "e p k h -> (e p) k h")).then_inc(wraw_ld[kind], 16)
                    sp.wait_ge(fw_lo, free)
                    sp.dma_start(raw[:, 2, :], w2r[bass.ds(it * (CH * P) + j * P, P), :]).then_inc(wraw_ld[2], 16)
            for t in range(TILES):
                first = TILES - TPB
                sp.wait_ge(*((out_ok, t + 1) if t < first else (out2_ok, t - first + 1)))
                sp.dma_start(out_tiles[t], acc[:, t, :]).then_inc(out_st, 16)
            sp.wait_ge(out_st, 16 * TILES)

        @block.gpsimd
        def _(pool):
            nc.gpsimd.memset(ident[:, :], 0.0).then_inc(id_step, 1)
            pool.wait_ge(id_step, 1)
            nc.gpsimd.affine_select(out=ident[:, :], in_=ident[:, :], compare_op=ALU.not_equal, fill=1.0, base=0,
                                    pattern=[[-1, P]], channel_multiplier=1).then_inc(id_step, 1)
            nc.gpsimd.memset(ones[:, :], 1.0).then_inc(pad_ok, 1)

            def one_like(src):
                one = ones[:, :].to_broadcast([P, BLK])
                return tiled(one) if len(src.shape) == 3 else one

            def split(n, src, hi, lo, hi_done, lo_done):
                nc.gpsimd.tensor_tensor(hi, src, one_like(src), ALU.mult).then_inc(hi_done, 1)
                pool.wait_ge(hi_done, n + 1)
                nc.gpsimd.tensor_tensor(lo, src, hi.bitcast(f32), ALU.subtract).then_inc(lo_done, 1)

            pool.wait_ge(pad_ok, 1)
            last_use = {w: max([k + 1 for k, (kind, m, _) in enumerate(JOBS) if (kind, m) == w] + [0]) for w in WORDER}
            for b in range(BATCH):
                for i, w in enumerate(WORDER):
                    n = NW * b + i
                    if n >= 2:
                        before, w2_ = divmod(n - 2, NW)
                        pool.wait_ge(pj_ps, NJ * before + last_use[WORDER[w2_]])
                    pool.wait_ge(raw_ld[n % 3], 16 * (n // 3 + 1))
                    ws = WS[n % 2]
                    split(n, tiled(raw[:, n % 3, :]), ws[:, 0], ws[:, 1], w_hi, w_lo)
                pool.wait_ge(crow_ok, 1)
                pool.wait_ge(xt_ps, TB * (b + 1))
                for t in range(TB):
                    g = TB * b + t
                    pool.wait_ge(x_ld[t], 16 * (2 * b + 1))
                    nc.gpsimd.tensor_tensor(acc[:, g, :], acc[:, g, :], crow[:, :], ALU.add).then_inc(xc_ok, 1)

            def split_chunk(cs, slot, arrived):
                for kind, dst in ((0, W1[slot]), (1, W3[slot]), (2, W2[slot])):
                    pool.wait_ge(wraw_ld[kind], arrived[kind])
                    src = raw[:, kind, :]
                    split(3 * cs + kind, tiled(src) if kind < 2 else src, dst[:, 0], dst[:, 1], fw_hi, fw_lo)

            pool.wait_ge(vc_ps, 2 * BATCH)
            nc.gpsimd.memset(below, 1.0).then_inc(below_ok, 1)
            pool.wait_ge(below_ok, 1)
            nc.gpsimd.affine_select(out=below, in_=below, compare_op=ALU.is_gt, fill=0.0, base=0,
                                    pattern=[[1, NE], [-1, NE]], channel_multiplier=0).then_inc(below_ok, 1)

            for c in range(SHC):
                if c == 0:
                    pool.wait_ge(fs_ps, TILES)
                if c == 2:
                    pool.wait_ge(fo_mm, TILES)
                if c == SHC - 1 and HSH % P:
                    pool.wait_ge(fw_lo, 3 * c)
                    for kind in range(2):
                        nc.gpsimd.memset(tiled(raw[:, kind, :])[:, :, HSH % P:P], 0.0).then_inc(pad_ok, 1)
                    pool.wait_ge(pad_ok, 3)
                    nc.gpsimd.memset(raw[HSH % P:P, 2, :], 0.0).then_inc(pad_ok, 1)
                    pool.wait_ge(pad_ok, 4)
                split_chunk(c, SH_SLOTS[c], [16 * (c + 1)] * 3)

            per_it = [sum(len(pieces(j)) for j in range(CH))] * 2 + [CH]
            with nc.gpsimd.Fori(0, ITERS) as it:
                sofar = [0, 0, 0]
                for gi, (first, slots) in enumerate(GROUPS):
                    done = it * ITU + (1, SHU, SHU + GROUPS[1][0] * NBLK, SHU + GROUPS[2][0] * NBLK)[gi]
                    pool.wait_ge(o_mm, done)
                    for c, slot in enumerate(slots):
                        n = len(pieces(first + c))
                        sofar = [sofar[0] + n, sofar[1] + n, sofar[2] + 1]
                        split_chunk(SHC + it * CH + first + c, slot,
                                    [it * (16 * per_it[k]) + 16 * (SHC + sofar[k]) for k in range(3)])

        @block.scalar
        def _(act):
            def hi_copy(ready, count, dst, src, done, bias=None):
                act.wait_ge(ready, count)
                if bias is None:
                    nc.scalar.activation(dst, src, ACT.Copy).then_inc(done, 1)
                else:
                    nc.scalar.activation(dst, src, ACT.Identity, bias=bias).then_inc(done, 1)

            def transposed_hi(n):
                hi_copy(xt_ps, n + 1, xt_dst(n)[0], tiled(bank(xt_bank(n))), xt_hi)

            def job_hi(b, k):
                q = NJ * b + k
                if JOBS[k][0] == "C":
                    if b:
                        act.wait_ge(vc_ps, 2 * b)
                    h = JOBS[k][2]
                    hi_copy(pj_ps, q + 1, VCT[:, h * BLK:h * BLK + BLK // 2], bank(2 + q % 2)[:, 0:BLK // 2], pj_hi)
                    return
                hi, _, bias = job_dst(*JOBS[k])
                if JOBS[k][:2] == ("Q", 1):
                    act.wait_ge(wvp_st, 32)
                hi_copy(pj_ps, q + 1, hi, bank(2 + q % 2), pj_hi, bias)

            act.wait_ge(bias_ld, 16)
            for b in range(BATCH):
                for h in range(NBB):
                    if b == 0:
                        for t in range(TPB):
                            transposed_hi(TPB * h + t)
                    job_hi(b, 2 * h)
                    job_hi(b, 2 * h + 1)
                job_hi(b, 4)
                job_hi(b, 5)
                if b == 0:
                    hi_copy(wvwp_ld, 32, WPR[:, 0], wp_raw, wp_hi)
                    hi_copy(gt_ps, 1, GWT[:, 0], bank(7)[:, 0:KD * NE].rearrange("p (k e) -> p k e", k=KD), gt_hi)
                    for k in range(KD):
                        hi_copy(wvt_ps, k + 1, WVT[:, 0, k, :], bank(k % 2), wvt_hi)
                    for k in range(KD):
                        hi_copy(wvp_ps, k + 1, WVP[0][:, k, :], bank(k % 2), wvp_hi)
                    act.wait_ge(lw_v, 1)
                    nc.scalar.activation(lw[:, 1:2], lw[:, 0:1], ACT.Exp, scale=-1.0).then_inc(lw_e, 1)
                else:
                    act.wait_ge(ve_ok, b)
                    s = slice(TB * (b - 1), TB * b)
                    nc.scalar.activation(rstd[:, 1, s], rstd[:, 0, s], ACT.Sqrt).then_inc(sq_ok, 1)
                for kind, n, i in CAM:
                    B = NBB * b + n
                    if kind == "F":
                        job_hi(b, i)
                    elif kind == "V":
                        hi_copy(vc_ps, 2 * b + i + 1, VC[:, 0, 4 * i:4 * i + 4, :], tiled(bank(4 + i)), vc_hi)
                    elif kind == "S":
                        g = TPB * B + i
                        act.wait_ge(bs_nm, g + 1)
                        if B == 0:
                            act.wait_ge(wp_lo, 1)
                        elif n:
                            act.wait_ge(bt_ps, TB * B)
                        nc.scalar.activation(base_p[:, i, :], bank(0, 2), ACT.Exp, bias=stat[:, 1, g:g + 1],
                                             scale=SCALE, accum_out=stat[:, 2, g:g + 1]).then_inc(bs_ex, 1)
                    elif kind == "T":
                        k = TB * B + i
                        if k >= 2:
                            act.wait_ge(bc_mm, k - 1)
                        elif k == 0:
                            act.wait_ge(crow_ps, 1)
                        hi_copy(bt_ps, k + 1, PTB[i % 2][:, 0, :], bank(4 + i % 2), bt_hi)
                    elif kind == "C" and i == TB - 1:
                        act.wait_ge(bc_mm, TB * (B + 1))
                        act.wait_ge(gbv_ok, 1)
                        if B:
                            act.wait_ge(qn_ok, B)
                        nc.scalar.activation(tcam, bank(6), ACT.Tanh, bias=gbv[:, 0:1], scale=gcol[:, 0:1]).then_inc(tc_ok, 1)
                        act.wait_ge(qn_ok, B + 1)
                        nc.scalar.activation(QT[:, 0, 0, n * BLK:(n + 1) * BLK], qfull, ACT.Copy).then_inc(qc_hi, 1)

                def exp_final(g):
                    i = g % TB
                    act.wait_ge(fs_nm, g + 1)
                    if i == 1:
                        act.wait_ge(qc_lo, NBB * (b + 1))
                    if i >= 2:
                        act.wait_ge(ft_ps, 2 * (g - 1))
                    nc.scalar.activation(final_p[:, i % 2, :], score_banks(i), ACT.Exp, bias=stat[:, 5, g:g + 1],
                                         scale=SCALE, accum_out=stat[:, 6, g:g + 1]).then_inc(fs_ex, 1)

                exp_final(TB * b)
                exp_final(TB * b + 1)
                for i in range(TB):
                    g = TB * b + i
                    for c in range(2):
                        hi_copy(ft_ps, 2 * g + c + 1, PTF[:, 0, 4 * c:4 * c + 4, :], tiled(bank(2 + c)), ft_hi)
                    transposed_hi(TB * (b + 1) + i)
                    if i + 2 < TB:
                        exp_final(g + 2)

            def logits_copy(nb):
                act.wait_ge(lg_ps, nb + 1)
                if nb >= 2:
                    act.wait_ge(lt_ps, nb - 1)
                nc.scalar.activation(ub[0:NE, 2 + nb % 2, :], bank(6 + nb % 2)[0:NE, :], ACT.Copy).then_inc(lg_cp, 1)

            def router_scores(nb):
                act.wait_ge(lt_ps, nb + 1)
                nc.scalar.activation(sc[:, 4 * nb:4 * nb + 4, :], bank(6 + nb % 2)[:, 0:TPB * NE].rearrange(
                    "p (t e) -> p t e", t=TPB), ACT.Sigmoid).then_inc(lg_sg, 1)

            logits_copy(0)
            logits_copy(1)
            act.wait_ge(ve_ok, BATCH)
            s = slice(TB * (BATCH - 1), TB * BATCH)
            nc.scalar.activation(rstd[:, 1, s], rstd[:, 0, s], ACT.Sqrt).then_inc(sq_ok, 1)
            router_scores(0)
            router_scores(1)
            for t in range(TB):
                transposed_hi(3 * TB + t)
            logits_copy(2)
            logits_copy(3)
            router_scores(2)
            router_scores(3)

            def spread(it, k):
                _, j, _, nb, _, _ = ORDER[k]
                for e, _, r, n in pieces(j):
                    src = router_dram[bass.ds(it * SB + e, 1), nb * BLK:(nb + 1) * BLK]
                    act.dma_start(pb[r:r + n, k % 4, :], src.to_broadcast([n, BLK])).then_inc(pb_ld[k % 4], 16)

            for u in range(SHU):
                act.wait_ge(h_mm, u + 1)
                if u >= 4:
                    act.wait_ge(hb_lo, u - 3)
                if u == 2:
                    act.wait_ge(lt_ps, NBLK)
                nc.scalar.activation(ub[:, u % 4, :], bank(2 * (u % 2)), ACT.Silu).then_inc(h1_cp, 1)
                act.wait_ge(h3_ok, u + 1)
                if u >= 2:
                    act.wait_ge(o_mm, u - 1)
                nc.scalar.activation(HB[u % 2][:, 0, :], ub[:, u % 4, :], ACT.Copy).then_inc(hb_hi, 1)
                if u >= PT_U:
                    nb = u - PT_U
                    act.wait_ge(pt_ps, nb + 1)
                    if nb:
                        act.wait_ge(pt_st, 16 * nb)
                    nc.scalar.activation(prT, bank(2 * ((nb + 1) % 2))[0:NE, :], ACT.Copy).then_inc(pt_cp, 1)
                    act.wait_ge(pt_cp, nb + 1)
                    act.dma_start(router_dram[:, nb * BLK:(nb + 1) * BLK], prT).then_inc(pt_st, 16)
            act.wait_ge(pt_st, 16 * NBLK)
            for k in range(4):
                spread(0, k)

            def iteration(it, final):
                for k in range(ITU):
                    u = it * ITU + (SHU + k)
                    act.wait_ge(h_mm, u + 1)
                    act.wait_ge(hb_lo, u - 3)
                    nc.scalar.activation(ub[:, k % 4, :], bank(2 * (k % 2)), ACT.Copy).then_inc(h1_cp, 1)
                    act.wait_ge(z_ok, it * ITU + (k + 1))
                    nc.scalar.activation(ub[:, k % 4, :], ub[:, k % 4, :], ACT.Silu).then_inc(silu_ok, 1)
                    act.wait_ge(h3_ok, u + 1)
                    act.wait_ge(o_mm, u - 1)
                    nc.scalar.activation(HB[k % 2][:, 0, :], ub[:, k % 4, :], ACT.Copy).then_inc(hb_hi, 1)
                    if k + 4 < ITU:
                        spread(it, k + 4)
                    elif not final:
                        spread(it + 1, k + 4 - ITU)

            with nc.scalar.Fori(0, ITERS - 1) as it:
                iteration(it, False)
            iteration(ITERS - 1, True)
            for n, s in enumerate((slice(0, TILES - TPB), slice(TILES - TPB, TILES))):
                act.wait_ge(ve_ok, BATCH + n + 1)
                nc.scalar.activation(rstd[:, 1, s], rstd[:, 0, s], ACT.Sqrt).then_inc(sq_ok, 1)
                if n == 0:
                    act.wait_ge(nm_ok, BATCH + 1)
                    for t in range(TILES - TPB):
                        nc.scalar.activation(acc[:, t, :], acc[:, t, :], ACT.Identity, bias=rstd[:, 0, t:t + 1],
                                             scale=rstd[:, 2, t:t + 1]).then_inc(out_ok, 1)

        @block.vector
        def _(dve):
            def lo_part(ready, count, dst, src, hi, done, bias=None):
                dve.wait_ge(ready, count)
                if bias is None:
                    nc.vector.tensor_tensor(dst, src, hi.bitcast(f32), ALU.subtract).then_inc(done, 1)
                else:
                    nc.vector.scalar_tensor_tensor(dst, src, bias, hi.bitcast(f32), ALU.add, ALU.subtract).then_inc(done, 1)

            def transposed_lo(n):
                hi, lo = xt_dst(n)
                lo_part(xt_hi, n + 1, lo, tiled(bank(xt_bank(n))), hi, xt_lo)

            def job_lo(b, k):
                q = NJ * b + k
                if JOBS[k][0] == "C":
                    if b:
                        dve.wait_ge(vc_ps, 2 * b)
                    h = JOBS[k][2]
                    dve.wait_ge(pj_hi, q + 1)
                    nc.vector.tensor_copy(VCT[:, h * BLK + BLK // 2:(h + 1) * BLK], bank(2 + q % 2)[:, BLK // 2:BLK]).then_inc(pj_lo, 1)
                    return
                hi, lo, bias = job_dst(*JOBS[k])
                lo_part(pj_hi, q + 1, lo, bank(2 + q % 2), hi, pj_lo, bias)

            def row_max(ready, g, row, mx, nm):
                dve.wait_ge(ready, g + 1)
                banks = score_banks(g % TB) if row else bank(0, 2)
                nc.vector.tensor_reduce(stat[:, row, g:g + 1], banks, AX.X, ALU.max).then_inc(mx, 1)
                dve.wait_ge(mx, g + 1)
                nc.vector.tensor_scalar(stat[:, row + 1, g:g + 1], stat[:, row, g:g + 1], -SCALE, None,
                                        ALU.mult).then_inc(nm, 1)

            def norm_scale(n, tiles, stats):
                dve.wait_ge(bag_ok, stats)
                nc.vector.tensor_scalar(rstd[:, 0, tiles], bag[:, tiles, 1], EPS, None, ALU.add).then_inc(ve_ok, 1)
                dve.wait_ge(sq_ok, n)
                nc.vector.reciprocal(rstd[:, 2, tiles], rstd[:, 1, tiles]).then_inc(rs_ok, 1)
                dve.wait_ge(rs_ok, n)
                nc.vector.scalar_tensor_tensor(rstd[:, 0, tiles], bag[:, tiles, 0], -1.0, rstd[:, 2, tiles], ALU.mult,
                                               ALU.mult).then_inc(nm_ok, 1)
                dve.wait_ge(nm_ok, n)

            def norm_tile(t, done):
                nc.vector.tensor_scalar(acc[:, t, :], acc[:, t, :], rstd[:, 2, t:t + 1], rstd[:, 0, t:t + 1],
                                        ALU.mult, ALU.add).then_inc(done, 1)

            dve.wait_ge(bias_ld, 16)
            bvb = bcol[:, 2 * KD:3 * KD].unsqueeze(2).to_broadcast([P, KD, P])
            nc.vector.tensor_copy(BVB[:, 0], bvb).then_inc(bvb_hi, 1)
            dve.wait_ge(bvb_hi, 1)
            nc.vector.tensor_tensor(BVB[:, 1], bvb, BVB[:, 0].bitcast(f32), ALU.subtract).then_inc(bvb_lo, 1)
            for b in range(BATCH):
                for h in range(NBB):
                    if b == 0:
                        for t in range(TPB):
                            transposed_lo(TPB * h + t)
                    job_lo(b, 2 * h)
                    job_lo(b, 2 * h + 1)
                job_lo(b, 4)
                job_lo(b, 5)
                if b == 0:
                    lo_part(wp_hi, 1, WPR[:, 1], wp_raw, WPR[:, 0], wp_lo)
                    lo_part(gt_hi, 1, GWT[:, 1], bank(7)[:, 0:KD * NE].rearrange("p (k e) -> p k e", k=KD), GWT[:, 0], gt_lo)
                    for k in range(KD):
                        lo_part(wvt_hi, k + 1, WVT[:, 1, k, :], bank(k % 2), WVT[:, 0, k, :], wvt_lo)
                    for k in range(KD):
                        lo_part(wvp_hi, k + 1, WVP[1][:, k, :], bank(k % 2), WVP[0][:, k, :], wvp_lo)
                    dve.wait_ge(const_ld, 16 * 6)
                    nc.vector.scalar_tensor_tensor(lw[:, 0:1], w1c[:, :], 0.5, w0c[:, :], ALU.mult, ALU.add).then_inc(lw_v, 1)
                    nc.vector.tensor_tensor(gbv[:, :], gcol[:, :], bcol[:, 2 * KD:2 * KD + 1], ALU.mult).then_inc(gbv_ok, 1)
                    dve.wait_ge(crow_ps, 1)
                    nc.vector.tensor_tensor(crow[:, :], bank(6), crow[:, :], ALU.add).then_inc(crow_ok, 1)
                    dve.wait_ge(lw_e, 1)
                    nc.vector.tensor_scalar(lw[:, 2:3], lw[:, 1:2], 1.0, None, ALU.add).then_inc(lw_v, 1)
                    dve.wait_ge(lw_v, 2)
                    nc.vector.reciprocal(lw[:, 3:4], lw[:, 2:3]).then_inc(lw_v, 1)
                else:
                    norm_scale(b, slice(TB * (b - 1), TB * b), TB * b)
                for kind, n, i in CAM:
                    B = NBB * b + n
                    s = slice(n * BLK, (n + 1) * BLK)
                    if kind == "F":
                        job_lo(b, i)
                    elif kind == "V":
                        lo_part(vc_hi, 2 * b + i + 1, VC[:, 1, 4 * i:4 * i + 4, :], tiled(bank(4 + i)),
                                VC[:, 0, 4 * i:4 * i + 4, :], vc_lo)
                    elif kind == "S":
                        g = TPB * B + i
                        row_max(bs_ps, g, 0, bs_mx, bs_nm)
                        dve.wait_ge(bs_ex, g + 1)
                        nc.vector.reciprocal(stat[:, 3, g:g + 1], stat[:, 2, g:g + 1]).then_inc(bs_ri, 1)
                        dve.wait_ge(bs_ri, g + 1)
                        nc.vector.tensor_scalar(base_p[:, i, :], base_p[:, i, :], stat[:, 3, g:g + 1], None,
                                                ALU.mult).then_inc(bs_no, 1)
                    elif kind == "T":
                        lo_part(bt_hi, TB * B + i + 1, PTB[i % 2][:, 1, :], bank(4 + i % 2), PTB[i % 2][:, 0, :], bt_lo)
                        if i == 0:
                            if B:
                                dve.wait_ge(qc_lo, B)
                            nc.vector.tensor_tensor(qfull, QT[:, 0, 0, s].bitcast(f32), QT[:, 1, 0, s].bitcast(f32),
                                                    ALU.add).then_inc(qf_ok, 1)
                    elif kind == "C" and b and n == 0 and i < TB - 1:
                        norm_tile(TB * (b - 1) + i, x1_ok)
                        if i == TB - 2:
                            norm_tile(TB * (b - 1) + i + 1, x1_ok)
                    elif kind == "C" and i == TB - 1:
                        dve.wait_ge(tc_ok, B + 1)
                        dve.wait_ge(qf_ok, B + 1)
                        if B == 0:
                            dve.wait_ge(lw_v, 3)
                        nc.vector.scalar_tensor_tensor(qfull, tcam, lw[:, 3:4], qfull, ALU.mult, ALU.add).then_inc(qn_ok, 1)
                        lo_part(qc_hi, B + 1, QT[:, 1, 0, s], qfull, QT[:, 0, 0, s], qc_lo)

                def residual(g):
                    dve.wait_ge(fo_mm, g + 1)
                    dve.wait_ge(xc_ok, g + 1)
                    dve.wait_ge(fs_ri, g + 1)
                    nc.vector.scalar_tensor_tensor(acc[:, g, :], bank(4 + g % 2), stat[:, 7, g:g + 1], acc[:, g, :],
                                                   ALU.mult, ALU.add).then_inc(res_ok, 1)
                    dve.wait_ge(res_ok, g + 1)
                    nc.vector.bn_stats(bst[:, g, :], acc[:, g, :]).then_inc(bst_ok, 1)
                    dve.wait_ge(bst_ok, g + 1)
                    nc.vector.bn_aggr(bag[:, g, :], bst[:, g, :]).then_inc(bag_ok, 1)

                row_max(fs_ps, TB * b, 4, fs_mx, fs_nm)
                row_max(fs_ps, TB * b + 1, 4, fs_mx, fs_nm)
                for i in range(TB):
                    g = TB * b + i
                    for c in range(2):
                        lo_part(ft_hi, 2 * g + c + 1, PTF[:, 1, 4 * c:4 * c + 4, :], tiled(bank(2 + c)),
                                PTF[:, 0, 4 * c:4 * c + 4, :], ft_lo)
                    dve.wait_ge(fs_ex, g + 1)
                    nc.vector.reciprocal(stat[:, 7, g:g + 1], stat[:, 6, g:g + 1]).then_inc(fs_ri, 1)
                    transposed_lo(TB * (b + 1) + i)
                    if i:
                        residual(g - 1)
                    if i + 2 < TB:
                        row_max(fs_ps, g + 2, 4, fs_mx, fs_nm)
                residual(TB * b + TB - 1)

            norm_scale(BATCH, slice(TB * (BATCH - 1), TB * BATCH), TILES)
            norm_tile(TB, x1_ok)
            norm_tile(TB + 1, x1_ok)
            for t in range(TB):
                if t + 2 < TB:
                    norm_tile(TB + t + 2, x1_ok)
                transposed_lo(3 * TB + t)

            steps = [0]

            def link(ins):
                steps[0] += 1
                ins.then_inc(rt_step, 1)
                dve.wait_ge(rt_step, steps[0])

            def rank_tiles(q):
                s4 = sc[:, 4 * q:4 * q + 4, :]
                other = s4.unsqueeze(2).to_broadcast([P, 4, NE, NE])
                own = s4.unsqueeze(3).to_broadcast([P, 4, NE, NE])
                if q == 0:
                    dve.wait_ge(lg_sg, NBLK)
                    dve.wait_ge(below_ok, 2)
                    link(nc.vector.tensor_tensor(sc, sc, gb[:, :].unsqueeze(1).to_broadcast([P, TILES, NE]), ALU.add))
                link(nc.vector.tensor_tensor(cmp_a_w, other, own, ALU.is_equal))
                link(nc.vector.tensor_tensor(cmp_a_w, cmp_a, below.unsqueeze(1).to_broadcast([P, 4, NE, NE]), ALU.mult))
                link(nc.vector.tensor_tensor(cmp_b_w, other, own, ALU.is_gt))
                link(nc.vector.tensor_tensor(cmp_a_w, cmp_a, cmp_b, ALU.add))
                link(nc.vector.tensor_reduce(rk[:, 4 * q:4 * q + 4, :], cmp_a, AX.X, ALU.add))

            def router_weights():
                link(nc.vector.tensor_scalar(rk, rk, float(TOPK), None, ALU.is_lt))
                link(nc.vector.tensor_tensor(pr, sc, rk, ALU.mult))
                link(nc.vector.tensor_reduce(wsum, pr, AX.X, ALU.add))
                link(nc.vector.reciprocal(winv, wsum))
                nc.vector.tensor_tensor(pr, pr, winv.unsqueeze(2).to_broadcast([P, TILES, NE]), ALU.mult).then_inc(pr_ok, 1)

            def evacuate(nb, before, units):
                dve.wait_ge(o_mm, units)
                if before is not None:
                    dve.wait_ge(acc_ok, before)
                for s in range(TPB):
                    t = nb * TPB + s
                    last = nc.vector.tensor_tensor(acc[:, t, :], bank(4 + s), acc[:, t, :], ALU.add)
                last.then_inc(acc_ok, 1)

            for u in range(SHU):
                nb, c = divmod(u, SHC)
                dve.wait_ge(h1_cp, u + 1)
                nc.vector.tensor_tensor(ub[:, u % 4, :], ub[:, u % 4, :], bank(2 * (u % 2) + 1), ALU.mult).then_inc(h3_ok, 1)
                lo_part(hb_hi, u + 1, HB[u % 2][:, 1, :], ub[:, u % 4, :], HB[u % 2][:, 0, :], hb_lo)
                if c == 0 and nb:
                    evacuate(nb - 1, nb - 1 if nb > 1 else None, u)
                if u in RANK_U:
                    rank_tiles(RANK_U.index(u))
                if u == RANK_U[-1] + 1:
                    router_weights()

            def final_stats(nb):
                for t in range(nb * TPB, (nb + 1) * TPB):
                    nc.vector.bn_stats(bst[:, t, :], acc[:, t, :]).then_inc(bst_ok, 1)
                for t in range(nb * TPB, (nb + 1) * TPB):
                    dve.wait_ge(bst_ok, TILES + t + 1)
                    nc.vector.bn_aggr(bag[:, t, :], bst[:, t, :]).then_inc(bag_ok, 1)

            def iteration(it, final):
                for k, (gi, _, _, nb, opens, _) in enumerate(ORDER):
                    u = it * ITU + (SHU + k)
                    dve.wait_ge(h1_cp, u + 1)
                    nc.vector.tensor_tensor(ub[:, k % 4, :], ub[:, k % 4, :], bank(2 * (k % 2) + 1),
                                            ALU.mult).then_inc(z_ok, 1)
                    dve.wait_ge(silu_ok, it * ITU + (k + 1))
                    dve.wait_ge(pb_ld[k % 4], it * (16 * PB_ALL[k % 4]) + 16 * PB_DMAS[k])
                    nc.vector.tensor_tensor(ub[:, k % 4, :], ub[:, k % 4, :], pb[:, k % 4, :], ALU.mult).then_inc(h3_ok, 1)
                    lo_part(hb_hi, u + 1, HB[k % 2][:, 1, :], ub[:, k % 4, :], HB[k % 2][:, 0, :], hb_lo)
                    if opens:
                        evacuate((nb - 1) % NBLK, it * BPI + (NBLK + gi * NBLK + nb - 1), u)
                        if final and gi == len(GROUPS) - 1 and nb:
                            dve.wait_ge(acc_ok, BPI * ITERS + nb)
                            final_stats(nb - 1)

            with nc.vector.Fori(0, ITERS - 1) as it:
                iteration(it, False)
            iteration(ITERS - 1, True)
            norm_scale(BATCH + 1, slice(0, TILES - TPB), 2 * TILES - TPB)
            dve.wait_ge(acc_ok, ITERS * BPI + NBLK - 1)
            for s in range(TPB):
                t = TILES - TPB + s
                dve.wait_ge(last_mm, s + 1)
                nc.vector.tensor_tensor(acc[:, t, :], bank(4 + s), acc[:, t, :], ALU.add).then_inc(last_ok, 1)
                dve.wait_ge(last_ok, s + 1)
                nc.vector.bn_stats(bst[:, t, :], acc[:, t, :]).then_inc(bst_ok, 1)
                dve.wait_ge(bst_ok, TILES + t + 1)
                nc.vector.bn_aggr(bag[:, t, :], bst[:, t, :]).then_inc(bag_ok, 1)
            norm_scale(BATCH + 2, slice(TILES - TPB, TILES), 2 * TILES)
            for t in range(TILES - TPB, TILES):
                norm_tile(t, out2_ok)

        @block.tensor
        def _(pe):
            def product(dst, lhs, rhs, first, last):
                for i, (a, b_) in enumerate(((0, 0), (0, 1), (1, 0))):
                    ins = nc.tensor.matmul(dst, lhs(a), rhs(b_), start=first and i == 0, stop=last and i == 2)
                return ins

            def transpose_tile(n, src):
                for k in range(KD):
                    ins = nc.tensor.transpose(bank(xt_bank(n))[:, k * P:(k + 1) * P], src[:, k * P:(k + 1) * P], ident[:, :])
                ins.then_inc(xt_ps, 1)

            def job(b, k, half=None):
                chunks = range(KD) if half is None else range(half * KD // 2, (half + 1) * KD // 2)
                q = NJ * b + k
                kind, m, h = JOBS[k]
                dst = bank(2 + q % 2)
                if q >= 2 and half != 1:
                    pe.wait_ge(pj_lo, q - 1)
                if kind == "V":
                    if m == 0 and half != 1:
                        pe.wait_ge(*((wvp_ld, 32) if b else (wvp_lo, KD)))
                    for c in chunks:
                        ins = product(dst, lambda i: XT[:, i, c, m * P:(m + 1) * P], lambda i: WVP[i][:, c, :],
                                      c == 0, c == KD - 1)
                else:
                    n = weight_no(b, kind, m)
                    if half != 1:
                        pe.wait_ge(w_lo, n + 1)
                        pe.wait_ge(xt_lo, TB * b + TPB * (h + 1))
                    for c in chunks:
                        ins = product(dst, lambda i: WS[n % 2][:, i, c, :], lambda i: XT[:, i, c, h * BLK:(h + 1) * BLK],
                                      c == 0, c == KD - 1)
                if half != 0:
                    ins.then_inc(pj_ps, 1)

            pe.wait_ge(id_step, 2)
            for b in range(BATCH):
                if b:
                    pe.wait_ge(ft_lo, 2 * TB * b)
                    pe.wait_ge(res_ok, TB * b)
                for h in range(NBB):
                    if b == 0:
                        for t in range(TPB * h, TPB * (h + 1)):
                            pe.wait_ge(x_ld[t], 16)
                            if t >= 2:
                                pe.wait_ge(xt_lo, t - 1)
                            transpose_tile(t, acc[:, t, :])
                    job(b, 2 * h)
                    job(b, 2 * h + 1)
                job(b, 4)
                job(b, 5)
                if b == 0:
                    def transpose_wv(ke):
                        if ke >= 2:
                            pe.wait_ge(wvt_lo, ke - 1)
                        for kd in range(KD):
                            ins = nc.tensor.transpose(bank(ke % 2)[:, kd * P:(kd + 1) * P], wv_raw[:, kd, ke * P:(ke + 1) * P],
                                                      ident[:, :])
                        ins.then_inc(wvt_ps, 1)

                    pe.wait_ge(wvwp_ld, 32)
                    transpose_wv(0)
                    transpose_wv(1)
                    pe.wait_ge(const_ld, 16 * 6)
                    pe.wait_ge(xt_lo, TB)
                    for k in range(KD):
                        ins = nc.tensor.transpose(bank(7)[:, k * NE:(k + 1) * NE], gw[:, k * P:(k + 1) * P], ident[0:NE, 0:NE])
                    ins.then_inc(gt_ps, 1)
                    pe.wait_ge(bvb_lo, 1)
                    pe.wait_ge(wp_lo, 1)
                    for ke in range(KD):
                        ins = product(bank(6), lambda i: BVB[:, i, ke, :], lambda i: WPR[:, i, ke, :], ke == 0, ke == KD - 1)
                    ins.then_inc(crow_ps, 1)
                    transpose_wv(2)
                    transpose_wv(3)
                    pe.wait_ge(wvt_lo, KD)
                    for kd in range(KD):
                        if kd >= 2:
                            pe.wait_ge(wvp_lo, kd - 1)
                        for ke in range(KD):
                            ins = product(bank(kd % 2), lambda i: WVT[:, i, ke, kd * P:(kd + 1) * P],
                                          lambda i: WPR[:, i, ke, :], ke == 0, ke == KD - 1)
                        ins.then_inc(wvp_ps, 1)
                    pe.wait_ge(wvp_lo, KD)

                for kind, n, i in CAM:
                    B = NBB * b + n
                    if kind in "fF":
                        job(b, i, "fF".index(kind))
                    elif kind == "V":
                        pe.wait_ge(pj_lo, NJ * b + len(HEAD))
                        for t in range(4):
                            ins = nc.tensor.transpose(bank(4 + i)[:, t * P:(t + 1) * P],
                                                      VCT[:, (4 * i + t) * P:(4 * i + t + 1) * P], ident[:, :])
                        ins.then_inc(vc_ps, 1)
                    elif kind == "S":
                        g = TPB * B + i
                        t = TPB * n + i
                        if n == 0 and i == 0:
                            pe.wait_ge(pj_lo, NJ * b + 4)
                        if g:
                            pe.wait_ge(bs_ex, g)
                        for h in range(2):
                            ins = product(bank(h), lambda p_: QT[:, p_, 0, t * P:(t + 1) * P],
                                          lambda p_: KT[:, p_, 0, h * BLK:(h + 1) * BLK], True, True)
                        ins.then_inc(bs_ps, 1)
                    elif kind == "T":
                        k = TB * B + i
                        if i == 0:
                            pe.wait_ge(vc_lo, 2 * (b + 1))
                        if k >= 2:
                            pe.wait_ge(bt_lo, k - 1)
                        for r in range(TPB):
                            if i == 0:
                                pe.wait_ge(bs_no, TPB * B + r + 1)
                            ins = nc.tensor.transpose(bank(4 + i % 2)[:, r * P:(r + 1) * P], base_p[:, r, i * P:(i + 1) * P],
                                                      ident[:, :])
                        ins.then_inc(bt_ps, 1)
                    else:
                        pe.wait_ge(bt_lo, TB * B + i + 1)
                        if i == 0:
                            pe.wait_ge(*((tc_ok, B) if B else (crow_ok, 1)))
                            pe.wait_ge(xt_lo, TB * (b + 1))
                        product(bank(6), lambda p_: VC[:, p_, i, :], lambda p_: PTB[i % 2][:, p_, :],
                                i == 0, i == TB - 1).then_inc(bc_mm, 1)

                def scores(g):
                    t = g % TB
                    pe.wait_ge(qc_lo, NBB * b + t // 4 + 1)
                    pe.wait_ge(pj_lo, NJ * (b + 1))
                    if t >= 2:
                        pe.wait_ge(fs_ex, g if t > 2 else g - 1)
                    for h in range(2):
                        for k in range(KD):
                            ins = product(score_banks(t)[:, h * BLK:(h + 1) * BLK], lambda p_: QT[:, p_, k, t * P:(t + 1) * P],
                                          lambda p_: KT[:, p_, k, h * BLK:(h + 1) * BLK], k == 0, k == KD - 1)
                    ins.then_inc(fs_ps, 1)

                scores(TB * b)
                scores(TB * b + 1)
                for i in range(TB):
                    g = TB * b + i
                    pe.wait_ge(fs_ex, g + 1)
                    for c in range(2):
                        if i:
                            pe.wait_ge(ft_lo, 2 * (g - 1) + c + 1)
                        for j in range(4):
                            tj = 4 * c + j
                            ins = nc.tensor.transpose(bank(2 + c)[:, j * P:(j + 1) * P],
                                                      final_p[:, i % 2, tj * P:(tj + 1) * P], ident[:, :])
                        ins.then_inc(ft_ps, 1)
                    n = TB * (b + 1) + i
                    pe.wait_ge(xt_lo, n - 1)
                    if b + 1 < BATCH:
                        pe.wait_ge(x_ld[i], 16 * 2)
                        if i == 0:
                            pe.wait_ge(tc_ok, NBB * (b + 1))
                        transpose_tile(n, acc[:, TB * (b + 1) + i, :])
                    else:
                        if i == 0:
                            pe.wait_ge(tc_ok, NBB * (b + 1))
                        pe.wait_ge(x1_ok, i + 1)
                        transpose_tile(n, acc[:, i, :])
                    if i + 2 < TB:
                        scores(g + 2)
                    if i == 0:
                        pe.wait_ge(fs_ex, g + 2)
                    if g >= 2:
                        pe.wait_ge(res_ok, g - 1)
                    for j in range(TB):
                        if j % 4 == 0:
                            pe.wait_ge(ft_lo, 2 * g + j // 4 + 1)
                        ins = product(bank(4 + g % 2), lambda p_: PTF[:, p_, j, :], lambda p_: VW[:, p_, j, :],
                                      j == 0, j == TB - 1)
                    ins.then_inc(fo_mm, 1)

            def x1t(i, k, nb):
                return X1T[nb // NBB][:, i, k, (nb % NBB) * BLK:(nb % NBB + 1) * BLK]

            def logits(nb):
                pe.wait_ge(xt_lo, TB * (BATCH + 1 + nb // NBB))
                if nb >= 2:
                    pe.wait_ge(lg_sg, nb - 1)
                for k in range(KD):
                    ins = product(bank(6 + nb % 2)[0:NE, :], lambda i: GWT[:, i, k, :], lambda i: x1t(i, k, nb),
                                  k == 0, k == KD - 1)
                ins.then_inc(lg_ps, 1)

            def logits_back(nb):
                pe.wait_ge(lg_cp, nb + 1)
                for s in range(TPB):
                    ins = nc.tensor.transpose(bank(6 + nb % 2)[:, s * NE:(s + 1) * NE],
                                              ub[0:NE, 2 + nb % 2, s * P:(s + 1) * P], ident[0:NE, 0:NE])
                ins.then_inc(lt_ps, 1)

            def hidden(slot, nb, par, between=None):
                for n, (w, bk) in enumerate(((W1, 2 * par), (W3, 2 * par + 1))):
                    for k in range(KD):
                        if between:
                            between(KD * n + k)
                        ins = product(bank(bk), lambda i: w[slot][:, i, k, :], lambda i: x1t(i, k, nb), k == 0, k == KD - 1)
                ins.then_inc(h_mm, 1)

            def down(slot, par, first, last, each=None):
                for s in range(TPB):
                    ins = product(bank(4 + s), lambda i: HB[par][:, i, s * P:(s + 1) * P], lambda i: W2[slot][:, i, :],
                                  first, last)
                    if each is not None:
                        ins.then_inc(each, 1)
                if each is None:
                    ins.then_inc(o_mm, 1)

            logits(0)
            logits(1)
            pe.wait_ge(fw_lo, 2)
            hidden(SH_SLOTS[0], 0, 0)
            logits_back(0)
            logits_back(1)

            def second_x1(t):
                pe.wait_ge(x1_ok, TB + t + 1)
                if t >= 2:
                    pe.wait_ge(xt_lo, 3 * TB + t - 1)
                transpose_tile(3 * TB + t, acc[:, TB + t, :])

            pe.wait_ge(res_ok, TILES)
            pe.wait_ge(fw_lo, 5)
            hidden(SH_SLOTS[1], 0, 1, second_x1)
            logits(2)
            logits(3)
            logits_back(2)
            logits_back(3)

            for u in range(SHU):
                nb, c = divmod(u, SHC)
                if nb == 0:
                    pe.wait_ge(fw_lo, 3 * c + 2)
                if u >= PT_U:
                    rnb = u - PT_U
                    pe.wait_ge(hb_lo, u)
                    pe.wait_ge(pr_ok, 1)
                    for s in range(TPB):
                        ins = nc.tensor.transpose(bank(2 * ((rnb + 1) % 2))[0:NE, s * P:(s + 1) * P],
                                                  pr[:, TPB * rnb + s, :], ident[:, :])
                    ins.then_inc(pt_ps, 1)
                if u:
                    if u >= PT_U + 1:
                        pe.wait_ge(pt_cp, u - PT_U)
                    if u >= 2:
                        hidden(SH_SLOTS[c], nb, u % 2)
                    pnb, pc = divmod(u - 1, SHC)
                    pe.wait_ge(hb_lo, u)
                    if u == 1:
                        pe.wait_ge(lg_sg, NBLK)
                    if pnb == 0:
                        pe.wait_ge(fw_lo, 3 * pc + 3)
                    if pc == 0 and pnb:
                        pe.wait_ge(acc_ok, pnb)
                    down(SH_SLOTS[pc], (u - 1) % 2, pc == 0, pc == SHC - 1)

            def iteration(it, final):
                for k, (gi, j, slot, nb, opens, closes) in enumerate(ORDER):
                    if nb == 0:
                        pe.wait_ge(fw_lo, it * (3 * CH) + 3 * (SHC + j + 1))
                    hidden(slot, nb, k % 2)
                    pe.wait_ge(hb_lo, it * ITU + (SHU + k))
                    if k == 0:
                        down(ORDER[-1][2], 1, False, True)
                    else:
                        pgi, _, pslot, pnb, popens, pcloses = ORDER[k - 1]
                        if popens:
                            pe.wait_ge(acc_ok, it * BPI + (NBLK + pgi * NBLK + pnb))
                        down(pslot, (k - 1) % 2, popens, pcloses)

            pe.wait_ge(pt_cp, NBLK)
            with nc.tensor.Fori(0, ITERS - 1) as it:
                iteration(it, False)
            iteration(ITERS - 1, True)
            pe.wait_ge(hb_lo, SHU + ITERS * ITU)
            down(ORDER[-1][2], 1, False, True, last_mm)


_INS = ['L0_attn_hidden_states', 'L0_attn_c_attn_w', 'L0_attn_c_attn_b', 'L0_attn_c_proj_w', 'L0_attn_c_proj_b',
        'L0_attn_cam_gate', 'L0_attn_cam_w0', 'L0_attn_cam_w1', 'L0_ffn_gate_w', 'L0_ffn_gate_b',
        'L0_ffn_w1_shared', 'L0_ffn_w2_shared', 'L0_ffn_w3_shared', 'L0_ffn_w1_routed', 'L0_ffn_w2_routed',
        'L0_ffn_w3_routed']


def kernel(**inputs):
    import numpy as _np
    import concourse.bacc as _bacc
    from concourse import mybir as _mybir
    from concourse.bass_utils import run_bass_kernel_spmd as _run

    nc = _bacc.Bacc("TRN2", target_bir_lowering=False, num_devices=1)
    arrays, args = {}, []
    for name in _INS:
        a = _np.ascontiguousarray(inputs[name])
        arrays[f"in_{name}_dram"] = a
        args.append(nc.dram_tensor(f"in_{name}_dram", a.shape, _mybir.dt.from_np(a.dtype), kind="ExternalInput").ap())
    fp32 = _mybir.dt.float32
    x_shape = inputs['L0_attn_hidden_states'].shape
    tokens = x_shape[0] * x_shape[1]
    width = x_shape[2]
    experts = inputs['L0_ffn_gate_w'].shape[0]
    args.append(nc.dram_tensor("router_weights_dram", (experts, tokens), fp32, kind="Internal").ap())
    chunks = width // 128
    args.append(nc.dram_tensor("value_projection_dram", (2, 128, chunks, width), fp32, kind="Internal").ap())
    args.append(nc.dram_tensor("out_0_dram", x_shape, fp32, kind="ExternalOutput").ap())
    post_ln_attention_moe_kernel(nc, *args)
    r = _run(nc, [arrays], core_ids=[0])
    return r.results[0]["out_0_dram"]
```

```python
import concourse.bass as bass
from concourse import mybir
from contextlib import ExitStack



def post_ln_attention_moe_kernel(
    nc, hidden_states, c_attn_w, c_attn_b, c_proj_w, c_proj_b, cam_gate, cam_w0, cam_w1,
    gate_w, gate_b, w1_shared, w2_shared, w3_shared, w1_routed, w2_routed, w3_routed,
    router_dram, vproj_dram, out,
):
    f32 = mybir.dt.float32
    f32r = mybir.dt.float32r
    ALU = mybir.AluOpType
    ACT = mybir.ActivationFunctionType
    AX = mybir.AxisListType

    P = 128
    BATCH, SEQ, D = hidden_states.shape
    KD = D // P
    TB = SEQ // P
    TILES = BATCH * TB
    BLK = 512
    TPB = BLK // P
    NBB = SEQ // BLK
    NBLK = BATCH * NBB
    DCAM = cam_gate.shape[0]
    SCALE = 1.0 / float(32) ** 0.5
    NE, _, HID = w1_routed.shape
    HSH = w1_shared.shape[1]
    TOPK = 4
    EPS = 1e-5
    assert DCAM == P

    SB = 4
    CH = SB * HID // P
    ITERS = NE // SB
    GROUPS = [(0, [0, 1]), (2, [3, 4, 5]), (5, [0, 1, 2]), (8, [3, 4, 5])]
    NSLOT = 6
    SHC = -(-HSH // P)
    PAD = SHC * P - HSH
    SH_SLOTS = [3, 4, 5]
    SHU = SHC * NBLK
    ITU = CH * NBLK
    assert NE <= PAD <= P

    def pieces(j):
        res, r = [], 0
        while r < P:
            e, c = divmod(P * j + r, HID)
            n = min(P - r, HID - c)
            res.append((e, c, r, n))
            r += n
        return res

    x_tiles = hidden_states.rearrange("b (t p) d -> (b t) p d", p=P)
    out_tiles = out.rearrange("b (t p) d -> (b t) p d", p=P)
    wqkv = c_attn_w.rearrange("(k p) n -> p k n", p=P)
    bqkv = c_attn_b.rearrange("(m p) -> p m", p=P)
    wp_v = c_proj_w.rearrange("(k p) n -> p k n", p=P)
    w1s = w1_shared.rearrange("(k p) h -> p k h", p=P)
    w3s = w3_shared.rearrange("(k p) h -> p k h", p=P)
    w1r = w1_routed.rearrange("e (k p) h -> e p k h", p=P)
    w3r = w3_routed.rearrange("e (k p) h -> e p k h", p=P)
    w2r = w2_routed.rearrange("e h d -> (e h) d")

    ctx = ExitStack()
    with ctx:
        def sb(name, shape, dt=f32):
            return ctx.enter_context(nc.sbuf_tensor(name, shape, dt))

        def sem(name):
            return ctx.enter_context(nc.semaphore(name))

        ps = ctx.enter_context(nc.psum_tensor("ps", [P, 8 * BLK], f32))

        def bank(i, n=1):
            return ps[:, i * BLK:(i + n) * BLK]

        R = sb("R", [P, 38 * 1024], f32r)
        acc = sb("acc", [P, TILES, D])
        scratch = sb("scratch", [P, 4 * BLK])
        raw = sb("raw", [P, 3, BLK])
        small = sb("small", [P, 2, BLK])
        crow = sb("crow", [P, D])
        GWT = sb("GWT", [P, KD, NE])
        ident = sb("ident", [P, P])
        bcol = sb("bcol", [P, 3 * KD])
        gcol = sb("gcol", [P, 1])
        gbv = sb("gbv", [P, 1])
        w0c = sb("w0c", [P, 1])
        w1c = sb("w1c", [P, 1])
        lw = sb("lw", [P, 4])
        ones = sb("ones", [P, 1])
        warm = sb("warm", [P, 1])
        stat = sb("stat", [P, 8, TILES])
        bst = sb("bst", [P, TILES, 6])
        bag = sb("bag", [P, TILES, 2])
        rstd = sb("rstd", [P, 3, TILES])
        gb = sb("gb", [P, NE])

        def view(off, *dims):
            n = 1
            for d in dims:
                n *= d
            v = R[:, off:off + n]
            if len(dims) == 2:
                return v.rearrange("p (a b) -> p a b", a=dims[0])
            return v.rearrange("p (a b c) -> p a b c", a=dims[0], b=dims[1])

        XT = view(0, 2, KD, SEQ)
        KT = view(8192, 2, KD, SEQ)
        QT = view(16384, 2, KD, SEQ)
        WVP = [R[:, 16384 + (1 + KD * i) * SEQ:16384 + (1 + KD * i) * SEQ + KD * D].rearrange("p (k n) -> p k n", k=KD)
               for i in range(2)]
        VW = view(24576, 2, TB, D)
        VC = view(32768, 2, TB, DCAM)
        PTF = view(32768, 2, TB, P)
        WS = [view(34816 + 1024 * s, 2, KD, P) for s in range(2)]
        PTB = [view(36864 + 1024 * s, 2, BLK) for s in range(2)]
        WVT = view(24576, 2, KD, D)
        WPR = view(28672, 2, KD, D)
        BVB = view(36864, 2, KD, P)
        X1T = [view(8192 * b, 2, KD, SEQ) for b in range(BATCH)]
        slot_at = [16384 + 3072 * ((s + 3) % NSLOT) for s in range(NSLOT)]
        W1 = [view(a, 2, KD, P) for a in slot_at]
        W3 = [view(a + 1024, 2, KD, P) for a in slot_at]
        W2 = [view(a + 2048, 2, D) for a in slot_at]
        HB = [view(34816 + 1024 * s, 2, BLK) for s in range(2)]
        pb = R[:, 36864:36864 + 4 * BLK].rearrange("p (s t) -> p s t", s=4).bitcast(f32)
        cmp_a_w = R[:, 36864:37888].rearrange("p (t e j) -> p t e j", t=TPB, e=NE)
        cmp_b_w = R[:, 37888:38912].rearrange("p (t e j) -> p t e j", t=TPB, e=NE)
        cmp_a, cmp_b = cmp_a_w.bitcast(f32), cmp_b_w.bitcast(f32)

        upper = acc[:, TB:2 * TB, :]
        base_p = upper.rearrange("p (s h) d -> p s (h d)", s=4)
        wv_raw = acc[:, TB:TB + KD, :]
        wp_raw = acc[:, TB + KD:TB + 2 * KD, :]
        final_p = scratch[:, :].rearrange("p (s t) -> p s t", s=2)
        tcam, qfull = scratch[:, 2 * BLK:3 * BLK], scratch[:, 3 * BLK:4 * BLK]
        gw = scratch[0:NE, 0:D]
        ub = scratch[:, :].rearrange("p (s t) -> p s t", s=4)
        sc = small[:, 1, 0:64].rearrange("p (t e) -> p t e", t=TPB)
        rk = small[:, 1, 64:128].rearrange("p (t e) -> p t e", t=TPB)
        pr = small[:, 1, 128:192].rearrange("p (t e) -> p t e", t=TPB)
        below = small[:, 1, 256:512].rearrange("p (e j) -> p e j", e=NE)
        prT = small[0:NE, 0, :]
        wsum = stat[:, 0, 0:TPB]
        winv = stat[:, 1, 0:TPB]

        bias_ld, const_ld, wvwp_ld = sem("bias_ld"), sem("const_ld"), sem("wvwp_ld")
        x_ld = [sem(f"x_ld{t}") for t in range(TB)]
        raw_ld = [sem(f"raw_ld{s}") for s in range(3)]
        id_step = sem("id_step")
        wp_hi, wp_lo = sem("wp_hi"), sem("wp_lo")
        w_hi, w_lo = sem("w_hi"), sem("w_lo")
        wvt_ps, wvt_hi, wvt_lo = sem("wvt_ps"), sem("wvt_hi"), sem("wvt_lo")
        bvb_hi, bvb_lo = sem("bvb_hi"), sem("bvb_lo")
        wvp_ps, wvp_hi, wvp_lo = sem("wvp_ps"), sem("wvp_hi"), sem("wvp_lo")
        wvp_st, wvp_ld = sem("wvp_st"), sem("wvp_ld")
        crow_ps, crow_ok = sem("crow_ps"), sem("crow_ok")
        lw_v, lw_e = sem("lw_v"), sem("lw_e")
        gbv_ok = sem("gbv_ok")
        xt_ps, xt_hi, xt_lo = sem("xt_ps"), sem("xt_hi"), sem("xt_lo")
        pj_ps, pj_hi, pj_lo = sem("pj_ps"), sem("pj_hi"), sem("pj_lo")
        vc_ps, vc_hi, vc_lo = sem("vc_ps"), sem("vc_hi"), sem("vc_lo")
        bs_ps, bs_mx, bs_nm, bs_ex, bs_ri, bs_no = (sem(f"bs_{n}") for n in ("ps", "mx", "nm", "ex", "ri", "no"))
        bt_ps, bt_hi, bt_lo, bc_mm = sem("bt_ps"), sem("bt_hi"), sem("bt_lo"), sem("bc_mm")
        tc_ok, qf_ok, qn_ok, qc_hi, qc_lo = sem("tc_ok"), sem("qf_ok"), sem("qn_ok"), sem("qc_hi"), sem("qc_lo")
        fs_ps, fs_mx, fs_nm, fs_ex, fs_ri = (sem(f"fs_{n}") for n in ("ps", "mx", "nm", "ex", "ri"))
        ft_ps, ft_hi, ft_lo, fo_mm = sem("ft_ps"), sem("ft_hi"), sem("ft_lo"), sem("fo_mm")
        xc_ok, res_ok, bst_ok, bag_ok = sem("xc_ok"), sem("res_ok"), sem("bst_ok"), sem("bag_ok")
        ve_ok, sq_ok, rs_ok, nm_ok, x1_ok = sem("ve_ok"), sem("sq_ok"), sem("rs_ok"), sem("nm_ok"), sem("x1_ok")
        gt_ps, gt_ok = sem("gt_ps"), sem("gt_ok")
        lg_cp, lt_ps, lg_sg = sem("lg_cp"), sem("lt_ps"), sem("lg_sg")
        rt_step, below_ok, pr_ok, pt_ps, pt_cp, pt_st = (sem(n) for n in ("rt_step", "below_ok", "pr_ok", "pt_ps", "pt_cp", "pt_st"))
        wraw_ld = [sem(f"wraw_ld{s}") for s in range(3)]
        pad_ok = sem("pad_ok")
        warm_ok = sem("warm_ok")
        fw_hi, fw_lo = sem("fw_hi"), sem("fw_lo")
        pb_ld = [sem(f"pb_ld{s}") for s in range(4)]
        h_mm, h1_cp, z_ok, silu_ok, h3_ok, hb_hi, hb_lo, o_mm, acc_ok = (
            sem(n) for n in ("h_mm", "h1_cp", "z_ok", "silu_ok", "h3_ok", "hb_hi", "hb_lo", "o_mm", "acc_ok"))
        last_mm, last_ok = sem("last_mm"), sem("last_ok")
        out_ok, out2_ok, out_st = sem("out_ok"), sem("out2_ok"), sem("out_st")

        HEAD = [("K", 0, 0), ("Q", 0, 0), ("K", 0, 1), ("Q", 0, 1), ("C", 0, 0), ("C", 0, 1)]
        FILL = ([("K", m, h) for m in range(1, KD) for h in range(NBB)] + [("V", t, 0) for t in range(TB)]
                + [("Q", m, h) for m in range(1, KD) for h in range(NBB)])
        JOBS = HEAD + FILL
        NJ = len(JOBS)
        CAM = []
        fill = len(HEAD)
        for n in range(NBB):
            for i in range(TPB):
                CAM += [("S", n, i), ("f", n, fill), ("F", n, fill)]
                fill += 1
                if n == 0 and i < 2:
                    CAM.append(("V", n, i))
            CAM += [("f", n, fill), ("F", n, fill), ("T", n, 0), ("f", n, fill + 1), ("F", n, fill + 1)]
            fill += 2
            for j in range(TB):
                if j + 1 < TB:
                    CAM.append(("T", n, j + 1))
                CAM += [("C", n, j), ("fF"[j % 2], n, fill)]
                fill += j % 2
        assert fill == NJ
        WORDER = [("K", 0), ("Q", 0), ("C", 0)] + [("K", m) for m in range(1, KD)] + [("Q", m) for m in range(1, KD)]
        NW = len(WORDER)
        assert NW % 3 == 0

        def weight_no(b, kind, m):
            return NW * b + WORDER.index((kind, m))

        VCT = small[:, :, :].rearrange("p a n -> p (a n)")

        def job_dst(kind, m, h):
            s = slice(h * BLK, (h + 1) * BLK)
            if kind == "K":
                return KT[:, 0, m, s], KT[:, 1, m, s], bcol[:, KD + m:KD + m + 1]
            if kind == "Q":
                return QT[:, 0, m, s], QT[:, 1, m, s], bcol[:, m:m + 1]
            return VW[:, 0, m, :], VW[:, 1, m, :], None

        def tiled(ap):
            return ap.rearrange("p (k t) -> p k t", k=KD)

        def xt_dst(n):
            b, t = divmod(n, TB)
            v = XT if b < BATCH else X1T[b - BATCH]
            return [v[:, i, :, t * P:(t + 1) * P] for i in range(2)]

        def xt_bank(n):
            return 6 + n % 2 if TB <= n < 3 * TB else 4 + n % 4

        def xt_free(n):
            return n - 1 if TB <= n < 3 * TB else max(n - 3, 0)

        def base_banks(g):
            return bank(6 * (g % 2), 2)

        def score_banks(i):
            return bank(4, 2) if i == 1 else bank(0, 2)

        def wv_bank(k):
            return (0, 1, 4, 5)[k]

        def shared_rows(c):
            return (PAD, 0) if c == 0 else (0, c * P - PAD)

        PT_UNITS = [SHC * (nb + 1) for nb in range(NBLK - 1)] + [SHU - 1]

        def left_bank(u):
            return bank(2 * ((u - 1) % 2) + 1)

        BPI = len(GROUPS) * NBLK
        ORDER = [(gi, first + c, slots[c], nb, c == 0, c == len(slots) - 1)
                 for gi, (first, slots) in enumerate(GROUPS) for nb in range(NBLK) for c in range(len(slots))]

        def unit_parts(final, k):
            if final and k == ITU - 1:
                return [slice(0, BLK // 2), slice(BLK // 2, BLK)]
            return [slice(0, BLK)]

        NORM_UNITS = [k for k, o in enumerate(ORDER) if o[0] == len(GROUPS) - 1 and o[3] and ORDER[k - 1][4]]
        LAST_PAIRS = [(TILES - 4, TILES - 3), (TILES - 2, TILES - 1)]
        PB_DMAS = [sum(len(pieces(ORDER[i][1])) for i in range(k % 4, k + 1, 4)) for k in range(ITU)]
        PB_ALL = [sum(len(pieces(ORDER[i][1])) for i in range(s, ITU, 4)) for s in range(4)]

        block = ctx.enter_context(nc.Block())

        @block.sync
        def _(sp):
            def load_x(b, t):
                sp.dma_start(acc[:, TB * b + t, :], x_tiles[TB * b + t]).then_inc(x_ld[t], 16)

            def load_raw(n):
                kind, m = WORDER[n % NW]
                col = {"Q": 0, "K": D, "C": 2 * D}[kind] + m * P
                if n >= 3:
                    sp.wait_ge(w_lo, n - 2)
                sp.dma_start(tiled(raw[:, n % 3, :]), wqkv[:, :, col:col + P]).then_inc(raw_ld[n % 3], 16)

            load_x(0, 0)
            load_x(0, 1)
            load_raw(0)
            for t in range(2, TPB):
                load_x(0, t)
            sp.dma_start(bcol[:, :], bqkv, allow_slow_non_contiguous=True).then_inc(bias_ld, 16)
            load_raw(1)
            for t in range(TPB, TB):
                load_x(0, t)
            load_raw(2)
            sp.dma_start(wv_raw, wqkv[:, :, 2 * D:3 * D]).then_inc(wvwp_ld, 16)
            sp.dma_start(wp_raw, wp_v).then_inc(wvwp_ld, 16)
            sp.dma_start(gw, gate_w).then_inc(const_ld, 16)
            sp.dma_start(gcol[:, :], cam_gate.rearrange("(p a) -> p a", a=1)).then_inc(const_ld, 16)
            sp.dma_start(w0c[:, :], cam_w0.rearrange("(a n) -> a n", a=1).to_broadcast([P, 1])).then_inc(const_ld, 16)
            sp.dma_start(w1c[:, :], cam_w1.rearrange("(a n) -> a n", a=1).to_broadcast([P, 1])).then_inc(const_ld, 16)
            sp.dma_start(crow[:, :], c_proj_b.rearrange("(a n) -> a n", a=1).to_broadcast([P, D])).then_inc(const_ld, 16)
            sp.dma_start(gb[:, :], gate_b.rearrange("(a n) -> a n", a=1).to_broadcast([P, NE])).then_inc(const_ld, 16)
            load_raw(3)
            load_raw(4)
            sp.wait_ge(wvp_lo, KD)
            for i in range(2):
                sp.dma_start(vproj_dram[i], WVP[i].bitcast(f32)).then_inc(wvp_st, 16)
            for n in range(5, NW):
                load_raw(n)
            sp.wait_ge(bt_ps, TB * NBB)
            for t in range(TB):
                load_x(1, t)
            for n in range(NW, NW + 3):
                load_raw(n)
            sp.wait_ge(fs_ps, TB)
            sp.wait_ge(wvp_st, 32)
            for i in range(2):
                sp.dma_start(WVP[i].bitcast(f32), vproj_dram[i]).then_inc(wvp_ld, 16)
            for n in range(NW + 3, 2 * NW):
                load_raw(n)
            sp.wait_ge(bt_ps, 2 * TB * NBB)
            for t in range(TB):
                load_x(1, t)

            for c in range(SHC):
                r, h = shared_rows(c)
                for kind, wsrc in ((0, w1s), (1, w3s)):
                    sp.wait_ge(*((fw_lo, 3 * c + kind - 2) if c else (w_lo, 2 * NW)))
                    sp.dma_start(tiled(raw[:, kind, :])[:, :, r:P], wsrc[:, :, h:h + P - r]).then_inc(wraw_ld[kind], 16)
                if c:
                    sp.wait_ge(fw_lo, 3 * c)
                sp.dma_start(raw[r:P, 2, :], w2_shared[h:h + P - r, :]).then_inc(wraw_ld[2], 16)

            with nc.sync.Fori(0, ITERS) as it:
                for j in range(CH):
                    free = it * (3 * CH) + 3 * (SHC + j)
                    for kind, wsrc in ((0, w1r), (1, w3r)):
                        sp.wait_ge(fw_lo, free + (kind - 2))
                        for e, c, r, n in pieces(j):
                            sp.dma_start(tiled(raw[:, kind, :])[:, :, r:r + n],
                                         wsrc[bass.ds(it * SB + e, 1), :, :, c:c + n].rearrange(
                                             "e p k h -> (e p) k h")).then_inc(wraw_ld[kind], 16)
                    sp.wait_ge(fw_lo, free)
                    sp.dma_start(raw[:, 2, :], w2r[bass.ds(it * (CH * P) + j * P, P), :]).then_inc(wraw_ld[2], 16)
            for t in range(TILES):
                first = TILES - TPB
                sp.wait_ge(*((out2_ok, t - first + 1) if first <= t < TILES - 1 else (out_ok, min(t, first) + 1)))
                sp.dma_start(out_tiles[t], acc[:, t, :]).then_inc(out_st, 16)
            sp.wait_ge(out_st, 16 * TILES)

        @block.gpsimd
        def _(pool):
            nc.gpsimd.memset(ident[:, :], 0.0).then_inc(id_step, 1)
            pool.wait_ge(id_step, 1)
            nc.gpsimd.affine_select(out=ident[:, :], in_=ident[:, :], compare_op=ALU.not_equal, fill=1.0, base=0,
                                    pattern=[[-1, P]], channel_multiplier=1).then_inc(id_step, 1)
            nc.gpsimd.memset(ones[:, :], 1.0).then_inc(pad_ok, 1)

            def one_like(src):
                one = ones[:, :].to_broadcast([P, BLK])
                return tiled(one) if len(src.shape) == 3 else one

            def split(n, src, hi, lo, hi_done, lo_done):
                nc.gpsimd.tensor_tensor(hi, src, one_like(src), ALU.mult).then_inc(hi_done, 1)
                pool.wait_ge(hi_done, n + 1)
                nc.gpsimd.tensor_tensor(lo, src, hi.bitcast(f32), ALU.subtract).then_inc(lo_done, 1)

            pool.wait_ge(pad_ok, 1)
            last_use = {w: max([k + 1 for k, (kind, m, _) in enumerate(JOBS) if (kind, m) == w] + [0]) for w in WORDER}
            for b in range(BATCH):
                for i, w in enumerate(WORDER):
                    n = NW * b + i
                    if n >= 2:
                        before, w2_ = divmod(n - 2, NW)
                        pool.wait_ge(pj_ps, NJ * before + last_use[WORDER[w2_]])
                    pool.wait_ge(raw_ld[n % 3], 16 * (n // 3 + 1))
                    ws = WS[n % 2]
                    split(n, tiled(raw[:, n % 3, :]), ws[:, 0], ws[:, 1], w_hi, w_lo)
                pool.wait_ge(crow_ok, 1)
                pool.wait_ge(xt_ps, TB * (b + 1))
                for t in range(TB):
                    g = TB * b + t
                    pool.wait_ge(x_ld[t], 16 * (2 * b + 1))
                    nc.gpsimd.tensor_tensor(acc[:, g, :], acc[:, g, :], crow[:, :], ALU.add).then_inc(xc_ok, 1)

            def split_chunk(cs, slot, arrived):
                for kind, dst in ((0, W1[slot]), (1, W3[slot]), (2, W2[slot])):
                    pool.wait_ge(wraw_ld[kind], arrived[kind])
                    src = raw[:, kind, :]
                    split(3 * cs + kind, tiled(src) if kind < 2 else src, dst[:, 0], dst[:, 1], fw_hi, fw_lo)

            pool.wait_ge(vc_ps, 2 * BATCH)
            nc.gpsimd.memset(below, 1.0).then_inc(below_ok, 1)
            pool.wait_ge(below_ok, 1)
            nc.gpsimd.affine_select(out=below, in_=below, compare_op=ALU.is_gt, fill=0.0, base=0,
                                    pattern=[[1, NE], [-1, NE]], channel_multiplier=0).then_inc(below_ok, 1)

            for c in range(SHC):
                if c == 0:
                    pool.wait_ge(fs_ps, TILES)
                if c == 2:
                    pool.wait_ge(fo_mm, TILES)
                if c == 0:
                    pool.wait_ge(w_lo, 2 * NW)
                    nc.gpsimd.memset(tiled(raw[:, 0, :])[:, :, NE:PAD], 0.0).then_inc(pad_ok, 1)
                    nc.gpsimd.memset(tiled(raw[:, 1, :])[:, :, 0:PAD], 0.0).then_inc(pad_ok, 1)
                    nc.gpsimd.memset(raw[0:PAD, 2, :], 0.0).then_inc(pad_ok, 1)
                    pool.wait_ge(gt_ok, 1)
                    nc.gpsimd.tensor_tensor(tiled(raw[:, 0, :])[:, :, 0:NE], GWT[:, :, :], ones[:, :].to_broadcast(
                        [P, KD * NE]).rearrange("p (k e) -> p k e", k=KD), ALU.mult).then_inc(pad_ok, 1)
                    pool.wait_ge(pad_ok, 5)
                split_chunk(c, SH_SLOTS[c], [16 * (c + 1)] * 3)

            per_it = [sum(len(pieces(j)) for j in range(CH))] * 2 + [CH]
            with nc.gpsimd.Fori(0, ITERS) as it:
                sofar = [0, 0, 0]
                for gi, (first, slots) in enumerate(GROUPS):
                    done = it * ITU + (1, SHU, SHU + GROUPS[1][0] * NBLK, SHU + GROUPS[2][0] * NBLK)[gi]
                    pool.wait_ge(o_mm, done)
                    for c, slot in enumerate(slots):
                        n = len(pieces(first + c))
                        sofar = [sofar[0] + n, sofar[1] + n, sofar[2] + 1]
                        split_chunk(SHC + it * CH + first + c, slot,
                                    [it * (16 * per_it[k]) + 16 * (SHC + sofar[k]) for k in range(3)])

        @block.scalar
        def _(act):
            def hi_copy(ready, count, dst, src, done, bias=None):
                act.wait_ge(ready, count)
                if bias is None:
                    nc.scalar.activation(dst, src, ACT.Copy).then_inc(done, 1)
                else:
                    nc.scalar.activation(dst, src, ACT.Identity, bias=bias).then_inc(done, 1)

            def transposed_hi(n):
                hi_copy(xt_ps, n + 1, xt_dst(n)[0], tiled(bank(xt_bank(n))), xt_hi)

            def job_hi(b, k):
                q = NJ * b + k
                if JOBS[k][0] == "C":
                    if b:
                        act.wait_ge(vc_ps, 2 * b)
                    h = JOBS[k][2]
                    hi_copy(pj_ps, q + 1, VCT[:, h * BLK:h * BLK + BLK // 2], bank(2 + q % 2)[:, 0:BLK // 2], pj_hi)
                    return
                hi, _, bias = job_dst(*JOBS[k])
                if JOBS[k][:2] == ("Q", 1):
                    act.wait_ge(wvp_st, 32)
                hi_copy(pj_ps, q + 1, hi, bank(2 + q % 2), pj_hi, bias)

            act.wait_ge(pad_ok, 1)
            nc.scalar.activation(warm[:, :], ones[:, :], ACT.Copy).then_inc(warm_ok, 1)
            for b in range(BATCH):
                if b == 0:
                    for t in range(TPB):
                        transposed_hi(t)
                    act.wait_ge(bias_ld, 16)
                job_hi(b, 0)
                if b == 0:
                    for t in range(TPB, TB):
                        transposed_hi(t)
                job_hi(b, 1)
                if b == 0:
                    hi_copy(wvwp_ld, 32, WPR[:, 0], wp_raw, wp_hi)
                job_hi(b, 2)
                if b == 0:
                    for k in range(2):
                        hi_copy(wvt_ps, k + 1, WVT[:, 0, k, :], bank(wv_bank(k)), wvt_hi)
                job_hi(b, 3)
                if b == 0:
                    for k in range(2, KD):
                        hi_copy(wvt_ps, k + 1, WVT[:, 0, k, :], bank(wv_bank(k)), wvt_hi)
                    hi_copy(gt_ps, 1, GWT[:, :, :], bank(7)[:, 0:KD * NE].rearrange("p (k e) -> p k e", k=KD), gt_ok)
                job_hi(b, 4)
                job_hi(b, 5)
                if b == 0:
                    for k in range(KD):
                        hi_copy(wvp_ps, k + 1, WVP[0][:, k, :], bank(wv_bank(k)), wvp_hi)
                    act.wait_ge(lw_v, 1)
                    nc.scalar.activation(lw[:, 1:2], lw[:, 0:1], ACT.Exp, scale=-1.0).then_inc(lw_e, 1)
                else:
                    act.wait_ge(ve_ok, b)
                    s = slice(TB * (b - 1), TB * b)
                    nc.scalar.activation(rstd[:, 1, s], rstd[:, 0, s], ACT.Sqrt).then_inc(sq_ok, 1)
                for kind, n, i in CAM:
                    B = NBB * b + n
                    if kind == "F":
                        job_hi(b, i)
                    elif kind == "V":
                        hi_copy(vc_ps, 2 * b + i + 1, VC[:, 0, 4 * i:4 * i + 4, :], tiled(bank(4 + i)), vc_hi)
                    elif kind == "S":
                        g = TPB * B + i
                        act.wait_ge(bs_nm, g + 1)
                        if B == 0:
                            act.wait_ge(wp_lo, 1)
                        elif n:
                            act.wait_ge(bt_ps, TB * B)
                        nc.scalar.activation(base_p[:, i, :], base_banks(g), ACT.Exp, bias=stat[:, 1, g:g + 1],
                                             scale=SCALE, accum_out=stat[:, 2, g:g + 1]).then_inc(bs_ex, 1)
                    elif kind == "T":
                        k = TB * B + i
                        if k >= 2:
                            act.wait_ge(bc_mm, k - 1)
                        elif k == 0:
                            act.wait_ge(crow_ps, 1)
                        hi_copy(bt_ps, k + 1, PTB[i % 2][:, 0, :], bank(4 + i % 2), bt_hi)
                    elif kind == "C" and i == TB - 1:
                        act.wait_ge(bc_mm, TB * (B + 1))
                        act.wait_ge(gbv_ok, 1)
                        if B:
                            act.wait_ge(qn_ok, B)
                        nc.scalar.activation(tcam, bank(6), ACT.Tanh, bias=gbv[:, 0:1], scale=gcol[:, 0:1]).then_inc(tc_ok, 1)
                        act.wait_ge(qn_ok, B + 1)
                        nc.scalar.activation(QT[:, 0, 0, n * BLK:(n + 1) * BLK], qfull, ACT.Copy).then_inc(qc_hi, 1)

                def exp_final(g):
                    i = g % TB
                    act.wait_ge(fs_nm, g + 1)
                    if i == 1:
                        act.wait_ge(qc_lo, NBB * (b + 1))
                    if i >= 2:
                        act.wait_ge(ft_ps, 2 * (g - 1))
                    nc.scalar.activation(final_p[:, i % 2, :], score_banks(i), ACT.Exp, bias=stat[:, 5, g:g + 1],
                                         scale=SCALE, accum_out=stat[:, 6, g:g + 1]).then_inc(fs_ex, 1)

                exp_final(TB * b)
                exp_final(TB * b + 1)
                for i in range(TB):
                    g = TB * b + i
                    for c in range(2):
                        hi_copy(ft_ps, 2 * g + c + 1, PTF[:, 0, 4 * c:4 * c + 4, :], tiled(bank(2 + c)), ft_hi)
                    transposed_hi(TB * (b + 1) + i)
                    if i + 2 < TB:
                        exp_final(g + 2)

            def shared_silu(u):
                nb, c = divmod(u, SHC)
                act.wait_ge(h_mm, u + 1)
                if u >= 4:
                    act.wait_ge(hb_lo, u - 3)
                if c == 2:
                    act.wait_ge(lt_ps, nb + 1)
                nc.scalar.activation(ub[:, u % 4, :], bank(2 * (u % 2)), ACT.Silu).then_inc(h1_cp, 1)
                if c == 0:
                    if u:
                        act.wait_ge(hb_lo, u - 1)
                    nc.scalar.activation(ub[0:NE, (u + 2) % 4, :], bank(2 * (u % 2))[0:NE, :], ACT.Copy).then_inc(lg_cp, 1)

            def shared_hi(u):
                act.wait_ge(h3_ok, u + 1)
                if u >= 2:
                    act.wait_ge(o_mm, u - 1)
                nc.scalar.activation(HB[u % 2][:, 0, :], ub[:, u % 4, :], ACT.Copy).then_inc(hb_hi, 1)

            def router_scores(nb):
                act.wait_ge(lt_ps, nb + 1)
                if nb:
                    act.wait_ge(pr_ok, nb)
                nc.scalar.activation(sc, left_bank(SHC * nb + 1)[:, 0:TPB * NE].rearrange("p (t e) -> p t e", t=TPB),
                                     ACT.Sigmoid).then_inc(lg_sg, 1)

            act.wait_ge(ve_ok, BATCH)
            s = slice(TB * (BATCH - 1), TB * BATCH)
            nc.scalar.activation(rstd[:, 1, s], rstd[:, 0, s], ACT.Sqrt).then_inc(sq_ok, 1)
            shared_silu(0)
            for t in range(TB):
                transposed_hi(3 * TB + t)
                if t == 0:
                    shared_hi(0)
                if t == TB - 2:
                    router_scores(0)

            def spread(it, k):
                _, j, _, nb, _, _ = ORDER[k]
                for e, _, r, n in pieces(j):
                    src = router_dram[bass.ds(it * SB + e, 1), nb * BLK:(nb + 1) * BLK]
                    act.dma_start(pb[r:r + n, k % 4, :], src.to_broadcast([n, BLK])).then_inc(pb_ld[k % 4], 16)

            for u in range(1, SHU):
                nb, c = divmod(u, SHC)
                if c == 1 and nb:
                    router_scores(nb)
                shared_silu(u)
                shared_hi(u)
                if u in PT_UNITS:
                    rnb = PT_UNITS.index(u)
                    act.wait_ge(pt_ps, rnb + 1)
                    if rnb:
                        act.wait_ge(pt_st, 16 * rnb)
                    nc.scalar.activation(prT, left_bank(u)[0:NE, :], ACT.Copy).then_inc(pt_cp, 1)
                    act.wait_ge(pt_cp, rnb + 1)
                    act.dma_start(router_dram[:, rnb * BLK:(rnb + 1) * BLK], prT).then_inc(pt_st, 16)
            ahead = max(ORDER[k][3] for k in range(4)) + 1
            act.wait_ge(pt_st, 16 * ahead)
            for k in range(4):
                spread(0, k)
            act.wait_ge(pt_st, 16 * NBLK)

            def root(n, tiles):
                act.wait_ge(ve_ok, n)
                nc.scalar.activation(rstd[:, 1, tiles], rstd[:, 0, tiles], ACT.Sqrt).then_inc(sq_ok, 1)

            def iteration(it, final):
                for k in range(ITU):
                    u = it * ITU + (SHU + k)
                    act.wait_ge(h_mm, u + 1)
                    act.wait_ge(hb_lo, u - 3)
                    parts = unit_parts(final, k)
                    for s in parts:
                        nc.scalar.activation(ub[:, k % 4, s], bank(2 * (k % 2))[:, s], ACT.Copy).then_inc(h1_cp, 1)
                    for i, s in enumerate(parts):
                        act.wait_ge(z_ok, it * ITU + (k + i + 1))
                        nc.scalar.activation(ub[:, k % 4, s], ub[:, k % 4, s], ACT.Silu).then_inc(silu_ok, 1)
                    act.wait_ge(o_mm, u - 1)
                    for i, s in enumerate(parts):
                        act.wait_ge(h3_ok, u + (i + 1))
                        nc.scalar.activation(HB[k % 2][:, 0, s], ub[:, k % 4, s], ACT.Copy).then_inc(hb_hi, 1)
                    if k + 4 < ITU:
                        spread(it, k + 4)
                    elif not final:
                        spread(it + 1, k + 4 - ITU)
                    if final and k in NORM_UNITS:
                        nb = NORM_UNITS.index(k)
                        root(BATCH + 1 + nb, slice(nb * TPB, (nb + 1) * TPB))
                        act.wait_ge(warm_ok, nb + 1)
                        nc.scalar.activation(warm[:, :], ones[:, :], ACT.Silu).then_inc(warm_ok, 1)

            with nc.scalar.Fori(0, ITERS - 1) as it:
                iteration(it, False)
            iteration(ITERS - 1, True)
            for n, pair in enumerate(LAST_PAIRS):
                if n == 0:
                    root(BATCH + NBLK, slice(pair[0], pair[-1] + 1))
                act.wait_ge(nm_ok, BATCH + NBLK + n)
                for t in pair:
                    if t < TILES - 1:
                        nc.scalar.activation(acc[:, t, :], acc[:, t, :], ACT.Identity, bias=rstd[:, 0, t:t + 1],
                                             scale=rstd[:, 2, t:t + 1]).then_inc(out2_ok, 1)
                    if t == LAST_PAIRS[0][0]:
                        root(BATCH + NBLK + 1, slice(LAST_PAIRS[1][0], LAST_PAIRS[1][-1] + 1))

        @block.vector
        def _(dve):
            def lo_part(ready, count, dst, src, hi, done, bias=None):
                dve.wait_ge(ready, count)
                if bias is None:
                    nc.vector.tensor_tensor(dst, src, hi.bitcast(f32), ALU.subtract).then_inc(done, 1)
                else:
                    nc.vector.scalar_tensor_tensor(dst, src, bias, hi.bitcast(f32), ALU.add, ALU.subtract).then_inc(done, 1)

            def transposed_lo(n):
                hi, lo = xt_dst(n)
                lo_part(xt_hi, n + 1, lo, tiled(bank(xt_bank(n))), hi, xt_lo)

            def job_lo(b, k):
                q = NJ * b + k
                if JOBS[k][0] == "C":
                    if b:
                        dve.wait_ge(vc_ps, 2 * b)
                    h = JOBS[k][2]
                    dve.wait_ge(pj_hi, q + 1)
                    nc.vector.tensor_copy(VCT[:, h * BLK + BLK // 2:(h + 1) * BLK], bank(2 + q % 2)[:, BLK // 2:BLK]).then_inc(pj_lo, 1)
                    return
                hi, lo, bias = job_dst(*JOBS[k])
                lo_part(pj_hi, q + 1, lo, bank(2 + q % 2), hi, pj_lo, bias)

            def row_max(ready, g, row, mx, nm):
                dve.wait_ge(ready, g + 1)
                banks = score_banks(g % TB) if row else base_banks(g)
                nc.vector.tensor_reduce(stat[:, row, g:g + 1], banks, AX.X, ALU.max).then_inc(mx, 1)
                dve.wait_ge(mx, g + 1)
                nc.vector.tensor_scalar(stat[:, row + 1, g:g + 1], stat[:, row, g:g + 1], -SCALE, None,
                                        ALU.mult).then_inc(nm, 1)

            def norm_variance(tiles, stats):
                dve.wait_ge(bag_ok, stats)
                nc.vector.tensor_scalar(rstd[:, 0, tiles], bag[:, tiles, 1], EPS, None, ALU.add).then_inc(ve_ok, 1)

            def norm_factors(n, tiles):
                dve.wait_ge(sq_ok, n)
                nc.vector.reciprocal(rstd[:, 2, tiles], rstd[:, 1, tiles]).then_inc(rs_ok, 1)
                dve.wait_ge(rs_ok, n)
                nc.vector.scalar_tensor_tensor(rstd[:, 0, tiles], bag[:, tiles, 0], -1.0, rstd[:, 2, tiles], ALU.mult,
                                               ALU.mult).then_inc(nm_ok, 1)
                dve.wait_ge(nm_ok, n)

            def norm_scale(n, tiles, stats):
                norm_variance(tiles, stats)
                norm_factors(n, tiles)

            def norm_tile(t, done):
                nc.vector.tensor_scalar(acc[:, t, :], acc[:, t, :], rstd[:, 2, t:t + 1], rstd[:, 0, t:t + 1],
                                        ALU.mult, ALU.add).then_inc(done, 1)

            for b in range(BATCH):
                if b == 0:
                    for t in range(TPB):
                        transposed_lo(t)
                    dve.wait_ge(bias_ld, 16)
                    bvb = bcol[:, 2 * KD:3 * KD].unsqueeze(2).to_broadcast([P, KD, P])
                    nc.vector.tensor_copy(BVB[:, 0], bvb).then_inc(bvb_hi, 1)
                    dve.wait_ge(bvb_hi, 1)
                    nc.vector.tensor_tensor(BVB[:, 1], bvb, BVB[:, 0].bitcast(f32), ALU.subtract).then_inc(bvb_lo, 1)
                job_lo(b, 0)
                if b == 0:
                    for t in range(TPB, TB):
                        transposed_lo(t)
                job_lo(b, 1)
                if b == 0:
                    lo_part(wp_hi, 1, WPR[:, 1], wp_raw, WPR[:, 0], wp_lo)
                job_lo(b, 2)
                if b == 0:
                    for k in range(2):
                        lo_part(wvt_hi, k + 1, WVT[:, 1, k, :], bank(wv_bank(k)), WVT[:, 0, k, :], wvt_lo)
                job_lo(b, 3)
                if b == 0:
                    for k in range(2, KD):
                        lo_part(wvt_hi, k + 1, WVT[:, 1, k, :], bank(wv_bank(k)), WVT[:, 0, k, :], wvt_lo)
                job_lo(b, 4)
                job_lo(b, 5)
                if b == 0:
                    for k in range(KD):
                        lo_part(wvp_hi, k + 1, WVP[1][:, k, :], bank(wv_bank(k)), WVP[0][:, k, :], wvp_lo)
                    dve.wait_ge(const_ld, 16 * 6)
                    nc.vector.scalar_tensor_tensor(lw[:, 0:1], w1c[:, :], 0.5, w0c[:, :], ALU.mult, ALU.add).then_inc(lw_v, 1)
                    nc.vector.tensor_tensor(gbv[:, :], gcol[:, :], bcol[:, 2 * KD:2 * KD + 1], ALU.mult).then_inc(gbv_ok, 1)
                    dve.wait_ge(crow_ps, 1)
                    nc.vector.tensor_tensor(crow[:, :], bank(6), crow[:, :], ALU.add).then_inc(crow_ok, 1)
                    dve.wait_ge(lw_e, 1)
                    nc.vector.tensor_scalar(lw[:, 2:3], lw[:, 1:2], 1.0, None, ALU.add).then_inc(lw_v, 1)
                    dve.wait_ge(lw_v, 2)
                    nc.vector.reciprocal(lw[:, 3:4], lw[:, 2:3]).then_inc(lw_v, 1)
                else:
                    norm_scale(b, slice(TB * (b - 1), TB * b), TB * b)
                def base_normalised(g):
                    dve.wait_ge(bs_ex, g + 1)
                    nc.vector.reciprocal(stat[:, 3, g:g + 1], stat[:, 2, g:g + 1]).then_inc(bs_ri, 1)
                    dve.wait_ge(bs_ri, g + 1)
                    nc.vector.tensor_scalar(base_p[:, g % TPB, :], base_p[:, g % TPB, :], stat[:, 3, g:g + 1], None,
                                            ALU.mult).then_inc(bs_no, 1)

                for kind, n, i in CAM:
                    B = NBB * b + n
                    s = slice(n * BLK, (n + 1) * BLK)
                    if kind == "F":
                        job_lo(b, i)
                    elif kind == "V":
                        lo_part(vc_hi, 2 * b + i + 1, VC[:, 1, 4 * i:4 * i + 4, :], tiled(bank(4 + i)),
                                VC[:, 0, 4 * i:4 * i + 4, :], vc_lo)
                    elif kind == "S":
                        g = TPB * B + i
                        row_max(bs_ps, g, 0, bs_mx, bs_nm)
                        if i:
                            base_normalised(g - 1)
                        if i == TPB - 1:
                            base_normalised(g)
                    elif kind == "T":
                        lo_part(bt_hi, TB * B + i + 1, PTB[i % 2][:, 1, :], bank(4 + i % 2), PTB[i % 2][:, 0, :], bt_lo)
                        if i == 0:
                            if B:
                                dve.wait_ge(qc_lo, B)
                            nc.vector.tensor_tensor(qfull, QT[:, 0, 0, s].bitcast(f32), QT[:, 1, 0, s].bitcast(f32),
                                                    ALU.add).then_inc(qf_ok, 1)
                    elif kind == "C" and b and n == 0 and i < TB - 1:
                        norm_tile(TB * (b - 1) + i, x1_ok)
                        if i == TB - 2:
                            norm_tile(TB * (b - 1) + i + 1, x1_ok)
                    elif kind == "C" and i == TB - 1:
                        dve.wait_ge(tc_ok, B + 1)
                        dve.wait_ge(qf_ok, B + 1)
                        if B == 0:
                            dve.wait_ge(lw_v, 3)
                        nc.vector.scalar_tensor_tensor(qfull, tcam, lw[:, 3:4], qfull, ALU.mult, ALU.add).then_inc(qn_ok, 1)
                        lo_part(qc_hi, B + 1, QT[:, 1, 0, s], qfull, QT[:, 0, 0, s], qc_lo)

                def residual(g):
                    dve.wait_ge(fo_mm, g + 1)
                    dve.wait_ge(xc_ok, g + 1)
                    dve.wait_ge(fs_ri, g + 1)
                    nc.vector.scalar_tensor_tensor(acc[:, g, :], bank(4 + g % 2), stat[:, 7, g:g + 1], acc[:, g, :],
                                                   ALU.mult, ALU.add).then_inc(res_ok, 1)
                    dve.wait_ge(res_ok, g + 1)
                    nc.vector.bn_stats(bst[:, g, :], acc[:, g, :]).then_inc(bst_ok, 1)
                    dve.wait_ge(bst_ok, g + 1)
                    nc.vector.bn_aggr(bag[:, g, :], bst[:, g, :]).then_inc(bag_ok, 1)

                row_max(fs_ps, TB * b, 4, fs_mx, fs_nm)
                row_max(fs_ps, TB * b + 1, 4, fs_mx, fs_nm)
                for i in range(TB):
                    g = TB * b + i
                    for c in range(2):
                        lo_part(ft_hi, 2 * g + c + 1, PTF[:, 1, 4 * c:4 * c + 4, :], tiled(bank(2 + c)),
                                PTF[:, 0, 4 * c:4 * c + 4, :], ft_lo)
                    dve.wait_ge(fs_ex, g + 1)
                    nc.vector.reciprocal(stat[:, 7, g:g + 1], stat[:, 6, g:g + 1]).then_inc(fs_ri, 1)
                    transposed_lo(TB * (b + 1) + i)
                    if i:
                        residual(g - 1)
                    if i + 2 < TB:
                        row_max(fs_ps, g + 2, 4, fs_mx, fs_nm)
                residual(TB * b + TB - 1)

            norm_scale(BATCH, slice(TB * (BATCH - 1), TB * BATCH), TILES)

            def shared_mul(u):
                dve.wait_ge(h1_cp, u + 1)
                nc.vector.tensor_tensor(ub[:, u % 4, :], ub[:, u % 4, :], bank(2 * (u % 2) + 1), ALU.mult).then_inc(h3_ok, 1)

            def shared_lo(u):
                lo_part(hb_hi, u + 1, HB[u % 2][:, 1, :], ub[:, u % 4, :], HB[u % 2][:, 0, :], hb_lo)

            for t in range(3):
                norm_tile(TB + t, x1_ok)
            shared_mul(0)
            for t in range(TB):
                if t + 3 < TB:
                    norm_tile(TB + t + 3, x1_ok)
                transposed_lo(3 * TB + t)
                if t == 0:
                    shared_lo(0)

            steps = [0]

            def link(ins):
                steps[0] += 1
                ins.then_inc(rt_step, 1)
                dve.wait_ge(rt_step, steps[0])

            def router_weights(nb):
                dve.wait_ge(lg_sg, nb + 1)
                dve.wait_ge(below_ok, 2)
                link(nc.vector.tensor_tensor(sc, sc, gb[:, :].unsqueeze(1).to_broadcast([P, TPB, NE]), ALU.add))
                other = sc.unsqueeze(2).to_broadcast([P, TPB, NE, NE])
                own = sc.unsqueeze(3).to_broadcast([P, TPB, NE, NE])
                link(nc.vector.tensor_tensor(cmp_a_w, other, own, ALU.is_equal))
                link(nc.vector.tensor_tensor(cmp_a_w, cmp_a, below.unsqueeze(1).to_broadcast([P, TPB, NE, NE]), ALU.mult))
                link(nc.vector.tensor_tensor(cmp_b_w, other, own, ALU.is_gt))
                link(nc.vector.tensor_tensor(cmp_a_w, cmp_a, cmp_b, ALU.add))
                link(nc.vector.tensor_reduce(rk, cmp_a, AX.X, ALU.add))
                link(nc.vector.tensor_scalar(rk, rk, float(TOPK), None, ALU.is_lt))
                if nb:
                    dve.wait_ge(pt_ps, nb)
                link(nc.vector.tensor_tensor(pr, sc, rk, ALU.mult))
                link(nc.vector.tensor_reduce(wsum, pr, AX.X, ALU.add))
                link(nc.vector.reciprocal(winv, wsum))
                nc.vector.tensor_tensor(pr, pr, winv.unsqueeze(2).to_broadcast([P, TPB, NE]), ALU.mult).then_inc(pr_ok, 1)

            def evacuate(nb, before, units):
                dve.wait_ge(o_mm, units)
                if before is not None:
                    dve.wait_ge(acc_ok, before)
                for s in range(TPB):
                    t = nb * TPB + s
                    last = nc.vector.tensor_tensor(acc[:, t, :], bank(4 + s), acc[:, t, :], ALU.add)
                last.then_inc(acc_ok, 1)

            for u in range(1, SHU):
                nb, c = divmod(u, SHC)
                shared_mul(u)
                shared_lo(u)
                if c == 0 and nb:
                    evacuate(nb - 1, nb - 1 if nb > 1 else None, u)
                if c == 1:
                    router_weights(nb)

            def final_stats(nb):
                for t in range(nb * TPB, (nb + 1) * TPB):
                    nc.vector.bn_stats(bst[:, t, :], acc[:, t, :]).then_inc(bst_ok, 1)
                for t in range(nb * TPB, (nb + 1) * TPB):
                    dve.wait_ge(bst_ok, TILES + t + 1)
                    nc.vector.bn_aggr(bag[:, t, :], bst[:, t, :]).then_inc(bag_ok, 1)

            def iteration(it, final):
                for k, (gi, _, _, nb, opens, _) in enumerate(ORDER):
                    u = it * ITU + (SHU + k)
                    parts = unit_parts(final, k)
                    for i, s in enumerate(parts):
                        dve.wait_ge(h1_cp, u + (i + 1))
                        nc.vector.tensor_tensor(ub[:, k % 4, s], ub[:, k % 4, s], bank(2 * (k % 2) + 1)[:, s],
                                                ALU.mult).then_inc(z_ok, 1)
                    dve.wait_ge(pb_ld[k % 4], it * (16 * PB_ALL[k % 4]) + 16 * PB_DMAS[k])
                    for i, s in enumerate(parts):
                        dve.wait_ge(silu_ok, it * ITU + (k + i + 1))
                        nc.vector.tensor_tensor(ub[:, k % 4, s], ub[:, k % 4, s], pb[:, k % 4, s], ALU.mult).then_inc(h3_ok, 1)
                    for i, s in enumerate(parts):
                        lo_part(hb_hi, u + (i + 1), HB[k % 2][:, 1, s], ub[:, k % 4, s], HB[k % 2][:, 0, s], hb_lo)
                    if opens:
                        evacuate((nb - 1) % NBLK, it * BPI + (NBLK + gi * NBLK + nb - 1), u)
                        if final and gi == len(GROUPS) - 1 and nb:
                            dve.wait_ge(acc_ok, BPI * ITERS + nb)
                            final_stats(nb - 1)
                            norm_variance(slice((nb - 1) * TPB, nb * TPB), TILES + nb * TPB)
                    if final and k in NORM_UNITS:
                        done = NORM_UNITS.index(k)
                        norm_factors(BATCH + 1 + done, slice(done * TPB, (done + 1) * TPB))
                        for t in range(done * TPB, (done + 1) * TPB):
                            norm_tile(t, out_ok)

            with nc.vector.Fori(0, ITERS - 1) as it:
                iteration(it, False)
            iteration(ITERS - 1, True)
            dve.wait_ge(acc_ok, ITERS * BPI + NBLK - 1)
            pairs = [slice(pair[0], pair[-1] + 1) for pair in LAST_PAIRS]
            for s in range(TPB + 2):
                t = TILES - TPB + s
                if s < TPB:
                    dve.wait_ge(last_mm, s + 1)
                    nc.vector.tensor_tensor(acc[:, t, :], bank(4 + s), acc[:, t, :], ALU.add).then_inc(last_ok, 1)
                if 1 <= s <= TPB:
                    dve.wait_ge(last_ok, s)
                    nc.vector.bn_stats(bst[:, t - 1, :], acc[:, t - 1, :]).then_inc(bst_ok, 1)
                if s >= 2:
                    dve.wait_ge(bst_ok, TILES + t - 1)
                    nc.vector.bn_aggr(bag[:, t - 2, :], bst[:, t - 2, :]).then_inc(bag_ok, 1)
                if s == TPB // 2 + 1:
                    norm_variance(pairs[0], 2 * TILES - TPB // 2)
                elif s == TPB // 2 + 2:
                    norm_factors(BATCH + NBLK, pairs[0])
            norm_variance(pairs[1], 2 * TILES)
            norm_factors(BATCH + NBLK + 1, pairs[1])
            norm_tile(TILES - 1, out_ok)

        @block.tensor
        def _(pe):
            def product(dst, lhs, rhs, first, last):
                for i, (a, b_) in enumerate(((0, 0), (0, 1), (1, 0))):
                    ins = nc.tensor.matmul(dst, lhs(a), rhs(b_), start=first and i == 0, stop=last and i == 2)
                return ins

            def transpose_tile(n, src):
                for k in range(KD):
                    ins = nc.tensor.transpose(bank(xt_bank(n))[:, k * P:(k + 1) * P], src[:, k * P:(k + 1) * P], ident[:, :])
                ins.then_inc(xt_ps, 1)

            def job(b, k, half=None):
                chunks = range(KD) if half is None else range(half * KD // 2, (half + 1) * KD // 2)
                q = NJ * b + k
                kind, m, h = JOBS[k]
                dst = bank(2 + q % 2)
                if q >= 2 and half != 1:
                    pe.wait_ge(pj_lo, q - 1)
                if kind == "V":
                    if m == 0 and half != 1:
                        pe.wait_ge(*((wvp_ld, 32) if b else (wvp_lo, KD)))
                    for c in chunks:
                        ins = product(dst, lambda i: XT[:, i, c, m * P:(m + 1) * P], lambda i: WVP[i][:, c, :],
                                      c == 0, c == KD - 1)
                else:
                    n = weight_no(b, kind, m)
                    if half != 1:
                        pe.wait_ge(w_lo, n + 1)
                        pe.wait_ge(xt_lo, TB * b + TPB * (h + 1))
                    for c in chunks:
                        ins = product(dst, lambda i: WS[n % 2][:, i, c, :], lambda i: XT[:, i, c, h * BLK:(h + 1) * BLK],
                                      c == 0, c == KD - 1)
                if half != 0:
                    ins.then_inc(pj_ps, 1)

            def x_transposed(tiles):
                for t in tiles:
                    pe.wait_ge(x_ld[t], 16)
                    if xt_free(t):
                        pe.wait_ge(xt_lo, xt_free(t))
                    transpose_tile(t, acc[:, t, :])

            def wv_transposed(ke):
                pe.wait_ge(wvwp_ld, 32)
                for kd in range(KD):
                    ins = nc.tensor.transpose(bank(wv_bank(ke))[:, kd * P:(kd + 1) * P], wv_raw[:, kd, ke * P:(ke + 1) * P],
                                              ident[:, :])
                ins.then_inc(wvt_ps, 1)

            pe.wait_ge(id_step, 2)
            for b in range(BATCH):
                if b:
                    pe.wait_ge(ft_lo, 2 * TB * b)
                else:
                    x_transposed(range(TPB))
                job(b, 0)
                if b == 0:
                    x_transposed(range(TPB, TB))
                job(b, 1)
                job(b, 2)
                if b == 0:
                    wv_transposed(0)
                    wv_transposed(1)
                job(b, 3)
                if b == 0:
                    wv_transposed(2)
                    wv_transposed(3)
                    pe.wait_ge(const_ld, 16 * 6)
                    for k in range(KD):
                        ins = nc.tensor.transpose(bank(7)[:, k * NE:(k + 1) * NE], gw[:, k * P:(k + 1) * P], ident[0:NE, 0:NE])
                    ins.then_inc(gt_ps, 1)
                job(b, 4)
                job(b, 5)
                if b == 0:
                    pe.wait_ge(bvb_lo, 1)
                    pe.wait_ge(wp_lo, 1)
                    for ke in range(KD):
                        ins = product(bank(6), lambda i: BVB[:, i, ke, :], lambda i: WPR[:, i, ke, :], ke == 0, ke == KD - 1)
                    ins.then_inc(crow_ps, 1)
                    pe.wait_ge(wvt_lo, KD)
                    for kd in range(KD):
                        for ke in range(KD):
                            ins = product(bank(wv_bank(kd)), lambda i: WVT[:, i, ke, kd * P:(kd + 1) * P],
                                          lambda i: WPR[:, i, ke, :], ke == 0, ke == KD - 1)
                        ins.then_inc(wvp_ps, 1)

                for kind, n, i in CAM:
                    B = NBB * b + n
                    if kind in "fF":
                        job(b, i, "fF".index(kind))
                    elif kind == "V":
                        pe.wait_ge(pj_lo, NJ * b + len(HEAD))
                        pe.wait_ge(*((res_ok, TB * b) if b else (wvp_lo, KD)))
                        for t in range(4):
                            ins = nc.tensor.transpose(bank(4 + i)[:, t * P:(t + 1) * P],
                                                      VCT[:, (4 * i + t) * P:(4 * i + t + 1) * P], ident[:, :])
                        ins.then_inc(vc_ps, 1)
                    elif kind == "S":
                        g = TPB * B + i
                        t = TPB * n + i
                        if n == 0 and i == 0:
                            pe.wait_ge(pj_lo, NJ * b + 4)
                        if g >= 2:
                            pe.wait_ge(bs_ex, g - 1)
                        else:
                            pe.wait_ge(*((crow_ok, 1) if g else (wvp_lo, 2)))
                        if g == 1:
                            pe.wait_ge(gt_ok, 1)
                        if i == 1:
                            pe.wait_ge(xt_lo, TB * (b + 1))
                            if B:
                                pe.wait_ge(tc_ok, B)
                        for h in range(2):
                            ins = product(base_banks(g)[:, h * BLK:(h + 1) * BLK], lambda p_: QT[:, p_, 0, t * P:(t + 1) * P],
                                          lambda p_: KT[:, p_, 0, h * BLK:(h + 1) * BLK], True, True)
                        ins.then_inc(bs_ps, 1)
                    elif kind == "T":
                        k = TB * B + i
                        if i == 0:
                            pe.wait_ge(vc_lo, 2 * (b + 1))
                        if k >= 2:
                            pe.wait_ge(bt_lo, k - 1)
                        for r in range(TPB):
                            if i == 0:
                                pe.wait_ge(bs_no, TPB * B + r + 1)
                            ins = nc.tensor.transpose(bank(4 + i % 2)[:, r * P:(r + 1) * P], base_p[:, r, i * P:(i + 1) * P],
                                                      ident[:, :])
                        ins.then_inc(bt_ps, 1)
                    else:
                        pe.wait_ge(bt_lo, TB * B + i + 1)
                        if i == 0:
                            pe.wait_ge(bs_ex, TPB * (B + 1))
                        product(bank(6), lambda p_: VC[:, p_, i, :], lambda p_: PTB[i % 2][:, p_, :],
                                i == 0, i == TB - 1).then_inc(bc_mm, 1)

                def scores(g):
                    t = g % TB
                    pe.wait_ge(qc_lo, NBB * b + t // 4 + 1)
                    pe.wait_ge(pj_lo, NJ * (b + 1) - (1 if t < TPB else 0))
                    if t == 0:
                        pe.wait_ge(bs_ex, TPB * NBB * (b + 1))
                    if t >= 2:
                        pe.wait_ge(fs_ex, g if t > 2 else g - 1)
                    for h in range(2):
                        for k in range(KD):
                            ins = product(score_banks(t)[:, h * BLK:(h + 1) * BLK], lambda p_: QT[:, p_, k, t * P:(t + 1) * P],
                                          lambda p_: KT[:, p_, k, h * BLK:(h + 1) * BLK], k == 0, k == KD - 1)
                    ins.then_inc(fs_ps, 1)

                def transpose_probs(g, c):
                    i = g % TB
                    pe.wait_ge(fs_ex, g + 1)
                    if i:
                        pe.wait_ge(ft_lo, 2 * (g - 1) + c + 1)
                    for j in range(4):
                        tj = 4 * c + j
                        ins = nc.tensor.transpose(bank(2 + c)[:, j * P:(j + 1) * P],
                                                  final_p[:, i % 2, tj * P:(tj + 1) * P], ident[:, :])
                    ins.then_inc(ft_ps, 1)

                def output_half(g, c):
                    pe.wait_ge(ft_lo, 2 * g + c + 1)
                    for j in range(4 * c, 4 * c + 4):
                        ins = product(bank(4 + g % 2), lambda p_: PTF[:, p_, j, :], lambda p_: VW[:, p_, j, :],
                                      j == 0, j == TB - 1)
                    return ins

                scores(TB * b)
                scores(TB * b + 1)
                transpose_probs(TB * b, 0)
                for i in range(TB):
                    g = TB * b + i
                    transpose_probs(g, 1)
                    n = TB * (b + 1) + i
                    pe.wait_ge(xt_lo, xt_free(n))
                    if i == 0:
                        pe.wait_ge(tc_ok, NBB * (b + 1))
                    if b + 1 < BATCH:
                        pe.wait_ge(x_ld[i], 16 * 2)
                        transpose_tile(n, acc[:, TB * (b + 1) + i, :])
                    else:
                        pe.wait_ge(x1_ok, i + 1)
                        transpose_tile(n, acc[:, i, :])
                    if i + 2 < TB:
                        scores(g + 2)
                    if i == 0:
                        pe.wait_ge(fs_ex, g + 2)
                    if g >= 2:
                        pe.wait_ge(res_ok, g - 1)
                    output_half(g, 0)
                    if i + 1 < TB:
                        transpose_probs(g + 1, 0)
                    output_half(g, 1).then_inc(fo_mm, 1)

            def x1t(i, k, nb):
                return X1T[nb // NBB][:, i, k, (nb % NBB) * BLK:(nb % NBB + 1) * BLK]

            def logits_back(nb):
                u = SHC * nb
                pe.wait_ge(lg_cp, nb + 1)
                for s in range(TPB):
                    ins = nc.tensor.transpose(left_bank(u + 1)[:, s * NE:(s + 1) * NE],
                                              ub[0:NE, (u + 2) % 4, s * P:(s + 1) * P], ident[0:NE, 0:NE])
                ins.then_inc(lt_ps, 1)

            def hidden(slot, nb, par, between=None):
                for n, (w, bk) in enumerate(((W1, 2 * par), (W3, 2 * par + 1))):
                    for k in range(KD):
                        if between:
                            between(KD * n + k)
                        ins = product(bank(bk), lambda i: w[slot][:, i, k, :], lambda i: x1t(i, k, nb), k == 0, k == KD - 1)
                ins.then_inc(h_mm, 1)

            def down(slot, par, first, last, each=None):
                for s in range(TPB):
                    if each is not None and s % 2 == 0:
                        pe.wait_ge(hb_lo, SHU + ITERS * ITU + s // 2)
                    ins = product(bank(4 + s), lambda i: HB[par][:, i, s * P:(s + 1) * P], lambda i: W2[slot][:, i, :],
                                  first, last)
                    if each is not None:
                        ins.then_inc(each, 1)
                if each is None:
                    ins.then_inc(o_mm, 1)

            pe.wait_ge(xt_lo, TB * (BATCH + 1))
            pe.wait_ge(fw_lo, 2)
            hidden(SH_SLOTS[0], 0, 0)

            def second_x1(t):
                pe.wait_ge(x1_ok, TB + t + 1)
                pe.wait_ge(xt_lo, xt_free(3 * TB + t))
                transpose_tile(3 * TB + t, acc[:, TB + t, :])
                if t == TB - 2:
                    pe.wait_ge(hb_lo, 1)
                    logits_back(0)

            pe.wait_ge(res_ok, TILES)
            pe.wait_ge(fw_lo, 5)
            hidden(SH_SLOTS[1], 0, 1, second_x1)
            pe.wait_ge(fw_lo, 8)
            pe.wait_ge(lg_sg, 1)
            hidden(SH_SLOTS[2], 0, 0)

            for u in range(1, SHU):
                nb, c = divmod(u, SHC)

                def small_things_read(n):
                    if n == KD and c == 2:
                        pe.wait_ge(lg_sg, nb + 1)
                    if n == KD and u - 1 in PT_UNITS:
                        pe.wait_ge(pt_cp, PT_UNITS.index(u - 1) + 1)

                if u >= SHC:
                    hidden(SH_SLOTS[c], nb, u % 2, small_things_read)
                pnb, pc = divmod(u - 1, SHC)
                pe.wait_ge(hb_lo, u)
                if c == 1 and nb:
                    logits_back(nb)
                if u == 1:
                    pe.wait_ge(xt_lo, TB * (BATCH + 2))
                if pnb == 0:
                    pe.wait_ge(fw_lo, 3 * pc + 3)
                if pc == 0 and pnb:
                    pe.wait_ge(acc_ok, pnb)
                down(SH_SLOTS[pc], (u - 1) % 2, pc == 0, pc == SHC - 1)
                if u in PT_UNITS:
                    rnb = PT_UNITS.index(u)
                    pe.wait_ge(pr_ok, rnb + 1)
                    for s in range(TPB):
                        ins = nc.tensor.transpose(left_bank(u)[0:NE, s * P:(s + 1) * P], pr[:, s, :], ident[:, :])
                    ins.then_inc(pt_ps, 1)

            def router_read(n):
                if n == KD:
                    pe.wait_ge(pt_cp, NBLK)

            def iteration(it):
                for k, (gi, j, slot, nb, _, _) in enumerate(ORDER):
                    if nb == 0:
                        pe.wait_ge(fw_lo, it * (3 * CH) + 3 * (SHC + j + 1))
                    hidden(slot, nb, k % 2, None if k else router_read)
                    pe.wait_ge(hb_lo, it * ITU + (SHU + k))
                    if k == 0:
                        down(ORDER[-1][2], 1, False, True)
                    else:
                        pgi, _, pslot, pnb, popens, pcloses = ORDER[k - 1]
                        if popens:
                            pe.wait_ge(acc_ok, it * BPI + (NBLK + pgi * NBLK + pnb))
                        down(pslot, (k - 1) % 2, popens, pcloses)

            with nc.tensor.Fori(0, ITERS - 1) as it:
                iteration(it)
            iteration(ITERS - 1)
            down(ORDER[-1][2], 1, False, True, last_mm)


_INS = ['L0_attn_hidden_states', 'L0_attn_c_attn_w', 'L0_attn_c_attn_b', 'L0_attn_c_proj_w', 'L0_attn_c_proj_b',
        'L0_attn_cam_gate', 'L0_attn_cam_w0', 'L0_attn_cam_w1', 'L0_ffn_gate_w', 'L0_ffn_gate_b',
        'L0_ffn_w1_shared', 'L0_ffn_w2_shared', 'L0_ffn_w3_shared', 'L0_ffn_w1_routed', 'L0_ffn_w2_routed',
        'L0_ffn_w3_routed']


def kernel(**inputs):
    import numpy as _np
    import concourse.bacc as _bacc
    from concourse import mybir as _mybir
    from concourse.bass_utils import run_bass_kernel_spmd as _run

    nc = _bacc.Bacc("TRN2", target_bir_lowering=False, num_devices=1)
    arrays, args = {}, []
    for name in _INS:
        a = _np.ascontiguousarray(inputs[name])
        arrays[f"in_{name}_dram"] = a
        args.append(nc.dram_tensor(f"in_{name}_dram", a.shape, _mybir.dt.from_np(a.dtype), kind="ExternalInput").ap())
    fp32 = _mybir.dt.float32
    x_shape = inputs['L0_attn_hidden_states'].shape
    tokens = x_shape[0] * x_shape[1]
    width = x_shape[2]
    experts = inputs['L0_ffn_gate_w'].shape[0]
    args.append(nc.dram_tensor("router_weights_dram", (experts, tokens), fp32, kind="Internal").ap())
    chunks = width // 128
    args.append(nc.dram_tensor("value_projection_dram", (2, 128, chunks, width), fp32, kind="Internal").ap())
    args.append(nc.dram_tensor("out_0_dram", x_shape, fp32, kind="ExternalOutput").ap())
    post_ln_attention_moe_kernel(nc, *args)
    r = _run(nc, [arrays], core_ids=[0])
    return r.results[0]["out_0_dram"]
```
